# Optimizing a Trainium2 kernel written in Bass

```python
import numpy as np
import jax
import jax.numpy as jnp

def _softmax(x, axis=-1):
    return jax.nn.softmax(x, axis=axis)

def _gelu(x):
    return jax.nn.gelu(x, approximate=True)

def _silu(x):
    return jax.nn.silu(x)

def _sigmoid(x):
    return jax.nn.sigmoid(x)

def _layernorm(x, axis=-1, eps=1e-05):
    m = jnp.mean(x, axis=axis, keepdims=True)
    v = jnp.var(x, axis=axis, keepdims=True)
    return (x - m) / jnp.sqrt(v + eps)

def _scatter_add(tgt, idx, src, axis=0):
    return tgt.at[idx].add(src)

def _segment_sum(src, seg, n):
    return jax.ops.segment_sum(src, seg, n)
kernel_name = 'mk_rec_standalone_d1_rec_r8_160dc5'

def setup_inputs(seed: int=0):
    np.random.seed(seed)
    _w = jnp.asarray

    def _rec_inputs():
        import jax
        import jax.numpy as jnp
        _rk = jax.random.key(seed)
        r_items = jnp.stack([jax.random.randint(jax.random.fold_in(jax.random.fold_in(_rk, 1), 0), (512,), 106, 99921, jnp.int32), jax.random.randint(jax.random.fold_in(jax.random.fold_in(_rk, 1), 1), (512,), 89, 99959, jnp.int32), jax.random.randint(jax.random.fold_in(jax.random.fold_in(_rk, 1), 2), (512,), 2, 99940, jnp.int32), jax.random.randint(jax.random.fold_in(jax.random.fold_in(_rk, 1), 3), (512,), 316, 99940, jnp.int32), jax.random.randint(jax.random.fold_in(jax.random.fold_in(_rk, 1), 4), (512,), 297, 12448, jnp.int32), jax.random.randint(jax.random.fold_in(jax.random.fold_in(_rk, 1), 5), (512,), 329, 99746, jnp.int32), jax.random.randint(jax.random.fold_in(jax.random.fold_in(_rk, 1), 6), (512,), 114, 12470, jnp.int32), jax.random.randint(jax.random.fold_in(jax.random.fold_in(_rk, 1), 7), (512,), 412, 99717, jnp.int32), jax.random.randint(jax.random.fold_in(jax.random.fold_in(_rk, 1), 8), (512,), 92, 99874, jnp.int32), jax.random.randint(jax.random.fold_in(jax.random.fold_in(_rk, 1), 9), (512,), 300, 99932, jnp.int32), jax.random.randint(jax.random.fold_in(jax.random.fold_in(_rk, 1), 10), (512,), 24, 99983, jnp.int32), jax.random.randint(jax.random.fold_in(jax.random.fold_in(_rk, 1), 11), (512,), 217, 99485, jnp.int32), jax.random.randint(jax.random.fold_in(jax.random.fold_in(_rk, 1), 12), (512,), 96, 99965, jnp.int32), jax.random.randint(jax.random.fold_in(jax.random.fold_in(_rk, 1), 13), (512,), 27, 99885, jnp.int32), jax.random.randint(jax.random.fold_in(jax.random.fold_in(_rk, 1), 14), (512,), 333, 99890, jnp.int32), jax.random.randint(jax.random.fold_in(jax.random.fold_in(_rk, 1), 15), (512,), 858, 99819, jnp.int32), jax.random.randint(jax.random.fold_in(jax.random.fold_in(_rk, 1), 16), (512,), 104, 99919, jnp.int32), jax.random.randint(jax.random.fold_in(jax.random.fold_in(_rk, 1), 17), (512,), 514, 99405, jnp.int32), jax.random.randint(jax.random.fold_in(jax.random.fold_in(_rk, 1), 18), (512,), 173, 99881, jnp.int32), jax.random.randint(jax.random.fold_in(jax.random.fold_in(_rk, 1), 19), (512,), 68, 99870, jnp.int32), jax.random.randint(jax.random.fold_in(jax.random.fold_in(_rk, 1), 20), (512,), 58, 12490, jnp.int32), jax.random.randint(jax.random.fold_in(jax.random.fold_in(_rk, 1), 21), (512,), 25, 99874, jnp.int32), jax.random.randint(jax.random.fold_in(jax.random.fold_in(_rk, 1), 22), (512,), 14, 99834, jnp.int32), jax.random.randint(jax.random.fold_in(jax.random.fold_in(_rk, 1), 23), (512,), 97, 99829, jnp.int32), jax.random.randint(jax.random.fold_in(jax.random.fold_in(_rk, 1), 24), (512,), 185, 99827, jnp.int32), jax.random.randint(jax.random.fold_in(jax.random.fold_in(_rk, 1), 25), (512,), 142, 99974, jnp.int32), jax.random.randint(jax.random.fold_in(jax.random.fold_in(_rk, 1), 26), (512,), 64, 12462, jnp.int32), jax.random.randint(jax.random.fold_in(jax.random.fold_in(_rk, 1), 27), (512,), 32, 99836, jnp.int32), jax.random.randint(jax.random.fold_in(jax.random.fold_in(_rk, 1), 28), (512,), 89, 99501, jnp.int32), jax.random.randint(jax.random.fold_in(jax.random.fold_in(_rk, 1), 29), (512,), 39, 99994, jnp.int32), jax.random.randint(jax.random.fold_in(jax.random.fold_in(_rk, 1), 30), (512,), 256, 99911, jnp.int32), jax.random.randint(jax.random.fold_in(jax.random.fold_in(_rk, 1), 31), (512,), 207, 99940, jnp.int32), jax.random.randint(jax.random.fold_in(jax.random.fold_in(_rk, 1), 32), (512,), 15, 99969, jnp.int32), jax.random.randint(jax.random.fold_in(jax.random.fold_in(_rk, 1), 33), (512,), 956, 12463, jnp.int32), jax.random.randint(jax.random.fold_in(jax.random.fold_in(_rk, 1), 34), (512,), 360, 12429, jnp.int32), jax.random.randint(jax.random.fold_in(jax.random.fold_in(_rk, 1), 35), (512,), 48, 99165, jnp.int32), jax.random.randint(jax.random.fold_in(jax.random.fold_in(_rk, 1), 36), (512,), 85, 99979, jnp.int32), jax.random.randint(jax.random.fold_in(jax.random.fold_in(_rk, 1), 37), (512,), 796, 12454, jnp.int32), jax.random.randint(jax.random.fold_in(jax.random.fold_in(_rk, 1), 38), (512,), 37, 99778, jnp.int32), jax.random.randint(jax.random.fold_in(jax.random.fold_in(_rk, 1), 39), (512,), 163, 99470, jnp.int32), jax.random.randint(jax.random.fold_in(jax.random.fold_in(_rk, 1), 40), (512,), 36, 99913, jnp.int32), jax.random.randint(jax.random.fold_in(jax.random.fold_in(_rk, 1), 41), (512,), 81, 99796, jnp.int32), jax.random.randint(jax.random.fold_in(jax.random.fold_in(_rk, 1), 42), (512,), 37, 99549, jnp.int32), jax.random.randint(jax.random.fold_in(jax.random.fold_in(_rk, 1), 43), (512,), 18, 99979, jnp.int32), jax.random.randint(jax.random.fold_in(jax.random.fold_in(_rk, 1), 44), (512,), 433, 99883, jnp.int32), jax.random.randint(jax.random.fold_in(jax.random.fold_in(_rk, 1), 45), (512,), 199, 12498, jnp.int32), jax.random.randint(jax.random.fold_in(jax.random.fold_in(_rk, 1), 46), (512,), 67, 99691, jnp.int32), jax.random.randint(jax.random.fold_in(jax.random.fold_in(_rk, 1), 47), (512,), 237, 99626, jnp.int32), jax.random.randint(jax.random.fold_in(jax.random.fold_in(_rk, 1), 48), (512,), 471, 99786, jnp.int32), jax.random.randint(jax.random.fold_in(jax.random.fold_in(_rk, 1), 49), (512,), 60, 99900, jnp.int32)], axis=1)
        r_inputs = jnp.stack([jax.random.randint(jax.random.fold_in(jax.random.fold_in(_rk, 2), 0), (512,), 49, 12494, jnp.int32), jax.random.randint(jax.random.fold_in(jax.random.fold_in(_rk, 2), 1), (512,), 171, 99937, jnp.int32), jax.random.randint(jax.random.fold_in(jax.random.fold_in(_rk, 2), 2), (512,), 51, 99789, jnp.int32), jax.random.randint(jax.random.fold_in(jax.random.fold_in(_rk, 2), 3), (512,), 91, 99950, jnp.int32), jax.random.randint(jax.random.fold_in(jax.random.fold_in(_rk, 2), 4), (512,), 19, 99927, jnp.int32), jax.random.randint(jax.random.fold_in(jax.random.fold_in(_rk, 2), 5), (512,), 306, 99709, jnp.int32), jax.random.randint(jax.random.fold_in(jax.random.fold_in(_rk, 2), 6), (512,), 183, 99941, jnp.int32), jax.random.randint(jax.random.fold_in(jax.random.fold_in(_rk, 2), 7), (512,), 277, 99862, jnp.int32), jax.random.randint(jax.random.fold_in(jax.random.fold_in(_rk, 2), 8), (512,), 1, 99886, jnp.int32), jax.random.randint(jax.random.fold_in(jax.random.fold_in(_rk, 2), 9), (512,), 179, 99173, jnp.int32), jax.random.randint(jax.random.fold_in(jax.random.fold_in(_rk, 2), 10), (512,), 206, 99930, jnp.int32), jax.random.randint(jax.random.fold_in(jax.random.fold_in(_rk, 2), 11), (512,), 57, 99945, jnp.int32), jax.random.randint(jax.random.fold_in(jax.random.fold_in(_rk, 2), 12), (512,), 7, 99593, jnp.int32), jax.random.randint(jax.random.fold_in(jax.random.fold_in(_rk, 2), 13), (512,), 9, 99854, jnp.int32), jax.random.randint(jax.random.fold_in(jax.random.fold_in(_rk, 2), 14), (512,), 51, 99906, jnp.int32), jax.random.randint(jax.random.fold_in(jax.random.fold_in(_rk, 2), 15), (512,), 769, 99243, jnp.int32), jax.random.randint(jax.random.fold_in(jax.random.fold_in(_rk, 2), 16), (512,), 192, 99799, jnp.int32), jax.random.randint(jax.random.fold_in(jax.random.fold_in(_rk, 2), 17), (512,), 249, 12468, jnp.int32), jax.random.randint(jax.random.fold_in(jax.random.fold_in(_rk, 2), 18), (512,), 154, 99961, jnp.int32), jax.random.randint(jax.random.fold_in(jax.random.fold_in(_rk, 2), 19), (512,), 58, 12489, jnp.int32), jax.random.randint(jax.random.fold_in(jax.random.fold_in(_rk, 2), 20), (512,), 213, 99457, jnp.int32), jax.random.randint(jax.random.fold_in(jax.random.fold_in(_rk, 2), 21), (512,), 290, 99972, jnp.int32), jax.random.randint(jax.random.fold_in(jax.random.fold_in(_rk, 2), 22), (512,), 130, 99748, jnp.int32), jax.random.randint(jax.random.fold_in(jax.random.fold_in(_rk, 2), 23), (512,), 197, 12485, jnp.int32), jax.random.randint(jax.random.fold_in(jax.random.fold_in(_rk, 2), 24), (512,), 74, 99939, jnp.int32), jax.random.randint(jax.random.fold_in(jax.random.fold_in(_rk, 2), 25), (512,), 101, 99988, jnp.int32), jax.random.randint(jax.random.fold_in(jax.random.fold_in(_rk, 2), 26), (512,), 228, 99559, jnp.int32), jax.random.randint(jax.random.fold_in(jax.random.fold_in(_rk, 2), 27), (512,), 532, 99886, jnp.int32), jax.random.randint(jax.random.fold_in(jax.random.fold_in(_rk, 2), 28), (512,), 208, 99692, jnp.int32), jax.random.randint(jax.random.fold_in(jax.random.fold_in(_rk, 2), 29), (512,), 255, 99932, jnp.int32), jax.random.randint(jax.random.fold_in(jax.random.fold_in(_rk, 2), 30), (512,), 9, 99850, jnp.int32), jax.random.randint(jax.random.fold_in(jax.random.fold_in(_rk, 2), 31), (512,), 454, 99977, jnp.int32), jax.random.randint(jax.random.fold_in(jax.random.fold_in(_rk, 2), 32), (512,), 73, 99922, jnp.int32), jax.random.randint(jax.random.fold_in(jax.random.fold_in(_rk, 2), 33), (512,), 258, 12477, jnp.int32), jax.random.randint(jax.random.fold_in(jax.random.fold_in(_rk, 2), 34), (512,), 27, 99494, jnp.int32), jax.random.randint(jax.random.fold_in(jax.random.fold_in(_rk, 2), 35), (512,), 164, 99406, jnp.int32), jax.random.randint(jax.random.fold_in(jax.random.fold_in(_rk, 2), 36), (512,), 13, 99883, jnp.int32), jax.random.randint(jax.random.fold_in(jax.random.fold_in(_rk, 2), 37), (512,), 109, 99773, jnp.int32), jax.random.randint(jax.random.fold_in(jax.random.fold_in(_rk, 2), 38), (512,), 70, 99563, jnp.int32), jax.random.randint(jax.random.fold_in(jax.random.fold_in(_rk, 2), 39), (512,), 136, 99982, jnp.int32), jax.random.randint(jax.random.fold_in(jax.random.fold_in(_rk, 2), 40), (512,), 39, 99997, jnp.int32), jax.random.randint(jax.random.fold_in(jax.random.fold_in(_rk, 2), 41), (512,), 243, 99948, jnp.int32), jax.random.randint(jax.random.fold_in(jax.random.fold_in(_rk, 2), 42), (512,), 167, 99275, jnp.int32), jax.random.randint(jax.random.fold_in(jax.random.fold_in(_rk, 2), 43), (512,), 387, 99981, jnp.int32), jax.random.randint(jax.random.fold_in(jax.random.fold_in(_rk, 2), 44), (512,), 193, 99949, jnp.int32), jax.random.randint(jax.random.fold_in(jax.random.fold_in(_rk, 2), 45), (512,), 12, 99422, jnp.int32), jax.random.randint(jax.random.fold_in(jax.random.fold_in(_rk, 2), 46), (512,), 38, 99941, jnp.int32), jax.random.randint(jax.random.fold_in(jax.random.fold_in(_rk, 2), 47), (512,), 27, 99546, jnp.int32), jax.random.randint(jax.random.fold_in(jax.random.fold_in(_rk, 2), 48), (512,), 63, 99676, jnp.int32), jax.random.randint(jax.random.fold_in(jax.random.fold_in(_rk, 2), 49), (512,), 1149, 99721, jnp.int32)], axis=1)
        r_alias_inputs = jax.random.randint(jax.random.fold_in(_rk, 3), (512, 50), 0, 50, jnp.int32)
        return (r_items, r_inputs, r_alias_inputs)
    r_items, r_inputs, r_alias_inputs = _rec_inputs()

    def _L0_rec_setup():
        import jax, jax.numpy as jnp
        import numpy as np
        NUM_NODE = 12500
        DIM = 128
        B = 512
        L = 50
        LAYERS = 2
        N_EDGES = 150000
        W_K = 12.0
        EPS = 1e-12

        def _l2norm(x):
            n = jnp.linalg.norm(x, axis=-1, keepdims=True)
            return x / jnp.maximum(n, EPS)
        key = jax.random.key(seed)
        ks = jax.random.split(key, 13)
        N = NUM_NODE + 1
        items = jax.random.randint(ks[0], (B, L), 0, N)
        inputs = jax.random.randint(ks[1], (B, L), 0, N)
        alias_inputs = jax.random.randint(ks[2], (B, L), 0, L)
        item_features = jax.random.normal(ks[3], (N, DIM), jnp.float32) * 0.02
        adj_row = jax.random.randint(ks[4], (N_EDGES,), 0, N)
        adj_col = jax.random.randint(ks[5], (N_EDGES,), 0, N)
        adj_val = jax.random.uniform(ks[6], (N_EDGES,), jnp.float32)
        stdv = 1.0 / np.sqrt(DIM)
        u = lambda k, s: jax.random.uniform(k, s, jnp.float32, -stdv, stdv)
        emb = u(ks[7], (N, DIM)).at[0].set(0.0)
        w_1 = u(ks[8], (2 * DIM, DIM))
        w_2 = u(ks[9], (DIM, 1))
        glu1_w = u(ks[10], (DIM, DIM))
        glu1_b = u(ks[11], (DIM,))
        glu2_w = u(ks[12], (DIM, DIM))
        return {'items': items, 'inputs': inputs, 'alias_inputs': alias_inputs, 'item_features': item_features, 'adj_row': adj_row, 'adj_col': adj_col, 'adj_val': adj_val, 'emb': emb, 'w_1': w_1, 'w_2': w_2, 'glu1_w': glu1_w, 'glu1_b': glu1_b, 'glu2_w': glu2_w}
    _L0_rec_all = _L0_rec_setup()
    _L0_rec_in = {k: v for k, v in _L0_rec_all.items() if k in ('item_features', 'adj_row', 'adj_col', 'adj_val', 'emb', 'w_1', 'w_2', 'glu1_w', 'glu1_b', 'glu2_w')}
    del _L0_rec_all
    return {'r_items': r_items, 'r_inputs': r_inputs, 'r_alias_inputs': r_alias_inputs, 'L0_rec_item_features': _L0_rec_in['item_features'], 'L0_rec_adj_row': _L0_rec_in['adj_row'], 'L0_rec_adj_col': _L0_rec_in['adj_col'], 'L0_rec_adj_val': _L0_rec_in['adj_val'], 'L0_rec_emb': _L0_rec_in['emb'], 'L0_rec_w_1': _L0_rec_in['w_1'], 'L0_rec_w_2': _L0_rec_in['w_2'], 'L0_rec_glu1_w': _L0_rec_in['glu1_w'], 'L0_rec_glu1_b': _L0_rec_in['glu1_b'], 'L0_rec_glu2_w': _L0_rec_in['glu2_w']}

def reference(r_items, r_inputs, r_alias_inputs, L0_rec_item_features, L0_rec_adj_row, L0_rec_adj_col, L0_rec_adj_val, L0_rec_emb, L0_rec_w_1, L0_rec_w_2, L0_rec_glu1_w, L0_rec_glu1_b, L0_rec_glu2_w):
    import jax
    import jax.numpy as jnp

    def _L0_rec_ref(items, inputs, alias_inputs, item_features, adj_row, adj_col, adj_val, emb, w_1, w_2, glu1_w, glu1_b, glu2_w):
        import jax, jax.numpy as jnp
        import numpy as np
        NUM_NODE = 12500
        DIM = 128
        B = 512
        L = 50
        LAYERS = 2
        N_EDGES = 150000
        W_K = 12.0
        EPS = 1e-12

        def _l2norm(x):
            n = jnp.linalg.norm(x, axis=-1, keepdims=True)
            return x / jnp.maximum(n, EPS)
        N = emb.shape[0]
        h = emb
        acc = emb
        for _ in range(LAYERS):
            h = jax.ops.segment_sum(adj_val[:, None] * h[adj_col], adj_row, num_segments=N)
            acc = acc + h
        graph_item_embs = acc / (LAYERS + 1)
        combined = graph_item_embs[items] + item_features[items]
        seq_hidden = jnp.take_along_axis(combined, alias_inputs[..., None], axis=1)
        mask = (inputs != 0)[..., None].astype(seq_hidden.dtype)
        hs = jnp.sum(seq_hidden * mask, axis=1) / jnp.sum(mask, axis=1)
        pos_emb = jnp.flip(emb[:L], axis=0)
        pos_b = jnp.broadcast_to(pos_emb[None], seq_hidden.shape)
        nh = jnp.tanh(jnp.concatenate([pos_b, seq_hidden], axis=-1) @ w_1)
        nh = jax.nn.sigmoid(nh @ glu1_w.T + glu1_b + (hs @ glu2_w.T)[:, None, :])
        beta = nh @ w_2 * mask
        sess_emb = jnp.sum(beta * seq_hidden, axis=1)
        select = W_K * _l2norm(sess_emb)
        scores = select @ _l2norm(graph_item_embs).T
        return scores
    y = _L0_rec_ref(r_items, r_inputs, r_alias_inputs, L0_rec_item_features, L0_rec_adj_row, L0_rec_adj_col, L0_rec_adj_val, L0_rec_emb, L0_rec_w_1, L0_rec_w_2, L0_rec_glu1_w, L0_rec_glu1_b, L0_rec_glu2_w)
    return y

_drawn_inputs = setup_inputs


def setup_inputs(seed=0):
    import zlib

    import numpy as np

    out = dict(_drawn_inputs(seed))
    spreads = {}
    factors = {'L0_rec_w_1': 3.923, 'L0_rec_glu1_w': 3.86, 'L0_rec_glu1_b': 28.586, 'L0_rec_glu2_w': 8.0}
    for name, (base, spread) in spreads.items():
        noise = np.random.default_rng([zlib.crc32(name.encode()), seed]).standard_normal(out[name].shape)
        drawn = base * np.exp(spread * noise) if base else spread * noise
        out[name] = jnp.asarray(drawn.astype(out[name].dtype))
    for name, factor in factors.items():
        out[name] = (out[name] * factor).astype(out[name].dtype)
    return out
```

```python
from contextlib import ExitStack

import concourse.bass as bass
from concourse import mybir

ALU = mybir.AluOpType
ACT = mybir.ActivationFunctionType
AX_X = mybir.AxisListType.X
F32 = mybir.dt.float32
BF16 = mybir.dt.bfloat16
I32 = mybir.dt.int32

P = 128
W_K = 12.0
EPS = 1e-12
LAYERS = 2


def ge(eng, sem, value):
    if isinstance(value, int) and value <= 0:
        return
    eng.wait_ge(sem, value)


def recommender_program(nc, items, inputs, alias, features, adj_row, adj_col, adj_val, emb,
                        w_1, w_2, glu1_w, glu1_b, glu2_w, out):
    B, L = items.shape
    N, D = emb.shape
    E = adj_row.shape[0]
    BT = B // P
    BUCKET = 256
    NB = -(-N // BUCKET)
    ROWS = NB * BUCKET
    COLS = E // P
    TAIL = E - COLS * P
    C = 8
    NCH = -(-(COLS + 1) // C)
    LAST = COLS + 1 - (NCH - 1) * C
    ECOLS = NCH * C
    NT = (E + NB * (P - 1)) // P
    T = 10
    NST = NT // T
    SR, PR = 10, 5
    assert NT % T == 0 and NST % 2 == 0 and NCH % 2 == 1 and D == P and 0 < TAIL < P
    LG = 4
    NG = -(-L // LG)
    NS = -(-N // 512)
    REM = N - (NS - 1) * 512
    TW = -(-NT // 3)

    with ExitStack() as ctx:
        def sb(name, shape, dt=F32):
            return ctx.enter_context(nc.sbuf_tensor(name, shape, dt))

        def sem(name):
            return ctx.enter_context(nc.semaphore(name))

        slots = nc.dram_tensor("sorted_edges", [P * NT, 4], F32).ap()
        table1 = nc.dram_tensor("table1", [ROWS, D], F32).ap()
        combined = nc.dram_tensor("combined", [ROWS, D], F32).ap()

        acc = sb("acc", [P, ROWS])
        big = sb("big", [P, ROWS])
        ring = sb("ring", [P, 2 * L * D])
        at = [0]

        def carve(base, words, dt=F32):
            v = base[:, at[0]:at[0] + words]
            at[0] += words
            return v if dt == F32 else v.bitcast(dt)

        e_row = carve(big, ECOLS, I32)
        e_col = carve(big, ECOLS, I32)
        e_val = carve(big, ECOLS)
        bkt_i = carve(big, ECOLS, I32)
        pay = carve(big, ECOLS * 4).rearrange("p (t w) -> p t w", w=4)
        bkt = carve(big, ECOLS // 2, BF16)
        eqm = carve(big, ECOLS // 2, BF16)
        eqj = carve(big, ECOLS // 2, BF16)
        eqk = carve(big, ECOLS // 2, BF16)
        assert at[0] <= ROWS
        at[0] = 0
        tile_iota = carve(ring, NT)
        tile_ge = carve(ring, NT // 2, BF16)
        at[0] = 0
        meta = carve(ring, NT * 4, F32)
        msg = carve(ring, 2 * T * D).rearrange("p (s d) -> p s d", d=D)
        onehot = carve(ring, SR * BUCKET).rearrange("p (s r) -> p s r", r=BUCKET)
        mring = carve(ring, 2 * T * 4)
        cring = carve(ring, 2 * T, I32)
        assert at[0] <= 2 * L * D
        at[0] = 0
        nh1 = carve(big, L * P)
        xT = carve(big, 2 * LG * P).rearrange("p (s n) -> p s n", s=2)
        ysum = carve(big, 2 * LG * P).rearrange("p (s n) -> p s n", s=2)
        nh2 = carve(big, 2 * LG * P).rearrange("p (s n) -> p s n", s=2)
        dmask = carve(big, 2 * LG * P).rearrange("p (s l n) -> p s l n", s=2, l=LG)
        hsT = carve(big, P)
        bias2 = carve(big, P)
        beta = carve(big, L)
        sess = carve(big, 4 * D).rearrange("p (s d) -> p s d", s=4)
        selT = carve(big, P)
        junk = carve(big, D)
        rown = carve(big, 8)
        assert at[0] <= ROWS
        seq = ring[:, :].rearrange("p (h l d) -> p h l d", h=2, l=L)

        ostage = sb("ostage", [P, 4, 512 * 2])
        gnr = sb("gnr", [P, 2, 2, D])
        ident = sb("ident", [P, P])
        ones = sb("ones", [P, P])
        onesb = sb("onesb", [P, P], BF16)
        lower = sb("lower", [P, P], BF16)
        zerob = sb("zerob", [P, P], BF16)
        iota_r = sb("iota_r", [P, BUCKET])
        iota_b = sb("iota_b", [P, NB])
        iota_bc = sb("iota_bc", [P, NB, C], BF16)
        iota_l = sb("iota_l", [P, L])
        gate = sb("gate", [P, 2])
        counts = sb("counts", [P, NB])
        toti = sb("toti", [P, NB], I32)
        toti2 = sb("toti2", [P, NB], I32)
        sqj = sb("sqj", [P, 2, D])
        rown0 = sb("rown0", [P, 1])
        ginv2 = sb("ginv2", [P, 2 * NB])
        ntile = sb("ntile", [P, NB])
        cum = sb("cum", [P, NB])
        start = sb("start", [P, NB])
        junkb = sb("junkb", [P, NB])
        startc = sb("startc", [P, 1])
        tile_off = sb("tile_off", [1, NT], I32)
        base = sb("base", [P, 2, NB])
        oh = sb("oh", [P, 2, NB, C], BF16)
        rank = sb("rank", [P, NB, C])
        posf = sb("posf", [P, C])
        posi = sb("posi", [P, C], I32)
        pos_p = sb("pos_p", [P, C], I32)
        pos_j = sb("pos_j", [P, C], I32)
        slot_i = sb("slot_i", [P, 2, C], I32)
        pring = sb("pring", [P, 2, C * 4])
        it_i = sb("it_i", [P, BT, L], I32)
        al_i = sb("al_i", [P, BT, L], I32)
        in_i = sb("in_i", [P, BT, L], I32)
        it_f = sb("it_f", [P, BT, L])
        it_n = sb("it_n", [P, BT, L])
        al_f = sb("al_f", [P, BT, L])
        mask = sb("mask", [P, BT, L])
        maskn = sb("maskn", [P, BT, L])
        mcnt = sb("mcnt", [P, BT])
        mrec = sb("mrec", [P, BT])
        sidf = sb("sidf", [P, L, BT])
        sidi = sb("sidi", [P, L, BT], I32)
        junkl = sb("junkl", [P, BT, L])
        ssq = sb("ssq", [P, 2 * NB])
        ginv = sb("ginv", [P, 2 * NB])
        w1a = sb("w1a", [D, D])
        w1b = sb("w1b", [D, D])
        w2c = sb("w2c", [D, 1])
        g1 = sb("g1", [D, D])
        g2 = sb("g2", [D, D])
        g1T = sb("g1T", [D, D])
        g2T = sb("g2T", [D, D])
        b1c = sb("b1c", [D, 1])
        erow = sb("erow", [L, D])
        eT = sb("eT", [D, L])
        posb = sb("posb", [D, L])

        bank = [ctx.enter_context(nc.psum_tensor(f"bank{i}", [P, 512], F32)) for i in range(8)]

        def octv(b):
            return bank[b][:, 0:NB * C].rearrange("p (b t) -> p b t", t=C)

        s_edge = sem("s_edge")
        s_sess = sem("s_sess")
        s_wts = sem("s_wts")
        s_cst = sem("s_cst")
        s_gate = sem("s_gate")
        s_init = sem("s_init")
        s_zero = sem("s_zero")
        s_v = sem("s_v")
        s_bkt = sem("s_bkt")
        s_eqm = sem("s_eqm")
        s_eqs = sem("s_eqs")
        s_cntv = sem("s_cntv")
        s_tot = sem("s_tot")
        s_tge = sem("s_tge")
        s_toff = sem("s_toff")
        s_oh = sem("s_oh")
        s_rank = sem("s_rank")
        s_rel = sem("s_rel")
        s_slot = sem("s_slot")
        s_sct = [sem(f"s_sct{h}") for h in range(2)]
        s_meta = sem("s_meta")
        s_mr = sem("s_mr")
        s_g = [sem(f"s_g{u}") for u in range(2 * T)]
        s_S = sem("s_S")
        s_mm = sem("s_mm")
        s_acc = sem("s_acc")
        s_t1 = sem("s_t1")
        s_t1a = sem("s_t1a")
        s_t1v = sem("s_t1v")
        s_t1w = sem("s_t1w")
        s_eld = sem("s_eld")
        s_fld = sem("s_fld")
        s_fz = sem("s_fz")
        s_t2 = sem("s_t2")
        s_g2r = sem("s_g2r")
        s_ssq = sem("s_ssq")
        s_cmb = sem("s_cmb")
        s_cw = sem("s_cw")
        s_wT = sem("s_wT")
        s_wTc = sem("s_wTc")
        s_pos = sem("s_pos")
        s_posc = sem("s_posc")
        s_nrm = sem("s_nrm")
        s_gi = sem("s_gi")
        s_gn = sem("s_gn")
        s_gnT = sem("s_gnT")
        s_gnc = sem("s_gnc")
        s_sid = sem("s_sid")
        s_sq = [sem(f"s_sq{i}") for i in range(2 * NG)]
        s_x = sem("s_x")
        s_xc = sem("s_xc")
        s_dm = sem("s_dm")
        s_z = sem("s_z")
        s_th = sem("s_th")
        s_hsc = sem("s_hsc")
        s_p2 = sem("s_p2")
        s_b2 = sem("s_b2")
        s_y = sem("s_y")
        s_ya = sem("s_ya")
        s_sg = sem("s_sg")
        s_bt = sem("s_bt")
        s_bm = sem("s_bm")
        s_ss = sem("s_ss")
        s_sn = sem("s_sn")
        s_sel = sem("s_sel")
        s_sT = sem("s_sT")
        s_sTc = sem("s_sTc")
        s_sc = sem("s_sc")
        s_sca = sem("s_sca")
        s_scv = sem("s_scv")
        s_out = [sem(f"s_out{i}") for i in range(4)]

        block = ctx.enter_context(nc.Block())
        GRP = 7
        assert NB % GRP == 0
        emb_full = N // P
        emb_rest = N - emb_full * P
        tab = [t.rearrange("(g p) d -> p g d", p=P) for t in (table1, combined)]
        big_rows = big[:, :].rearrange("p (g d) -> p g d", d=D)
        acc_rows = acc[:, :].rearrange("p (g d) -> p g d", d=D)
        feat_rows = ring[:, 0:ROWS].rearrange("p (g d) -> p g d", d=D)
        HALVES = (NCH + 1) // 2, NCH // 2

        @block.sync
        def _(sp):
            sp.wait_ge(s_init, 3)
            for n, (dst, src) in enumerate(((e_row, adj_row), (e_col, adj_col), (e_val, adj_val))):
                sp.dma_start(dst[:, 0:COLS], src[0:COLS * P].rearrange("(p t) -> p t", t=COLS)).then_inc(s_edge, 16)
                sp.dma_start(dst[0:TAIL, COLS:COLS + 1],
                             src[COLS * P:E].rearrange("(p t) -> p t", t=1)).then_inc(s_edge, 16)
            sp.wait_ge(s_cst, 1)
            sp.dma_start(slots.rearrange("(p j) w -> p (j w)", p=P), acc[:, 0:NT * 4]).then_inc(s_zero, 16)
            for h in range(2):
                full = HALVES[h] if h != (NCH - 1) % 2 else HALVES[h] - 1
                sp.wait_ge(s_sct[h], 16 * (C * full + (LAST if h == (NCH - 1) % 2 else 0)))
            sp.wait_ge(s_toff, 3)
            sp.dma_start(meta, slots.rearrange("(p j) w -> p (j w)", p=P)).then_inc(s_meta, 16)
            for r in range(NB // GRP):
                sp.wait_ge(s_t1a, (GRP * (r + 1) + 1) // 2)
                sp.wait_ge(s_t1v, (GRP * (r + 1)) // 2)
                a, b = 2 * GRP * r, 2 * GRP * (r + 1)
                sp.dma_start(tab[0][:, a:b, :], big_rows[:, a:b, :]).then_inc(s_t1w, 16)
            sp.wait_ge(s_t1w, 16 * (NB // GRP))
            sp.dma_start(big_rows[:, 0:emb_full, :],
                         emb[0:emb_full * P, :].rearrange("(g p) d -> p g d", p=P)).then_inc(s_eld, 16)
            sp.wait_ge(s_fz, 1)
            sp.dma_start(big_rows[0:emb_rest, emb_full, :], emb[emb_full * P:N, :]).then_inc(s_eld, 16)
            sp.wait_ge(s_fz, 2)
            sp.dma_start(feat_rows[0:emb_rest, emb_full, :], features[emb_full * P:N, :]).then_inc(s_fld, 16)
            sp.dma_start(feat_rows[:, 0:emb_full, :],
                         features[0:emb_full * P, :].rearrange("(g p) d -> p g d", p=P)).then_inc(s_fld, 16)
            for r in range(NB // GRP):
                sp.wait_ge(s_cmb, GRP * (r + 1))
                a, b = 2 * GRP * r, 2 * GRP * (r + 1)
                sp.dma_start(tab[1][:, a:b, :], big_rows[:, a:b, :]).then_inc(s_cw, 16)
            for bt in range(BT):
                for q in range(-(-NS // 2)):
                    m = (-(-NS // 2)) * bt + q
                    sp.wait_ge(s_sca, m + 1)
                    if 2 * q + 1 < NS:
                        sp.wait_ge(s_scv, (NS // 2) * bt + q + 1)
                    a, b = 1024 * q, min(1024 * q + 1024, N)
                    sp.dma_start(out[bt * P:(bt + 1) * P, a:b], ostage[:, m % 4, 0:b - a]).then_inc(s_out[m % 4], 16)
            total = (-(-NS // 2)) * BT
            for i in range(4):
                sp.wait_ge(s_out[i], 16 * ((total - i + 3) // 4))

        @block.gpsimd
        def _(pool):
            pool.memset(acc[:, :], 0.0).then_inc(s_cst, 1)
            pool.memset(gate[:, :], 0.0).then_inc(s_gate, 1)
            pool.memset(ones[:, :], 1.0).then_inc(s_cst, 1)
            pool.memset(ident[:, :], 0.0).then_inc(s_cst, 1)
            pool.memset(onesb[:, :], 1.0).then_inc(s_cst, 1)
            pool.memset(zerob[:, :], 0.0).then_inc(s_cst, 1)
            pool.iota(iota_r[:, :], [[1, BUCKET]], base=0, channel_multiplier=0,
                      allow_small_or_imprecise_dtypes=True).then_inc(s_cst, 1)
            pool.iota(iota_b[:, :], [[1, NB]], base=0, channel_multiplier=0,
                      allow_small_or_imprecise_dtypes=True).then_inc(s_cst, 1)
            pool.iota(iota_bc[:, :, :], [[1, NB], [0, C]], base=0, channel_multiplier=0,
                      allow_small_or_imprecise_dtypes=True).then_inc(s_cst, 1)
            pool.iota(iota_l[:, :], [[1, L]], base=0, channel_multiplier=0,
                      allow_small_or_imprecise_dtypes=True).then_inc(s_cst, 1)
            pool.iota(tile_iota[:, :], [[1, NT]], base=0, channel_multiplier=0,
                      allow_small_or_imprecise_dtypes=True).then_inc(s_cst, 1)
            pool.wait_ge(s_cst, 10)
            pool.affine_select(out=ident[:, :], in_=ident[:, :], compare_op=ALU.not_equal, fill=1.0, base=0,
                               pattern=[[-1, P]], channel_multiplier=1).then_inc(s_cst, 1)
            pool.affine_select(out=lower[:, :], in_=onesb[:, :], compare_op=ALU.is_gt, fill=0.0, base=0,
                               pattern=[[1, P]], channel_multiplier=-1).then_inc(s_cst, 1)

            def opened(n, waits):
                pool.wait_ge(s_gate, n + 1)
                for s, v in waits:
                    ge(pool, s, v)
                pool.tensor_tensor(gate[:, 0:1], gate[:, 1:2], gate[:, 1:2], ALU.add).then_inc(s_gate, 1)

            def scatter_step(c, h, n):
                opened(c, [(s_slot, c + 1)])
                for t in range(n):
                    k = TAIL if n == LAST and t == LAST - 1 else P
                    pool.indirect_dma_start(slots, bass.IndirectOffsetOnAxis(slot_i[0:k, h, t:t + 1], 0),
                                            pring[0:k, h, 4 * t:4 * t + 4], None).then_inc(s_sct[h], 16)

            pool.wait_ge(s_zero, 16)
            with pool.Fori(0, NCH // 2) as i:
                for h in range(2):
                    scatter_step(2 * i + h, h, C)
            scatter_step(NCH - 1, (NCH - 1) % 2, LAST)

            def gather_step(layer, source, c, h):
                opened(NCH + NST * layer + c, [(s_mr, NST * layer + c + 1)] +
                       ([(s_mm, NT * layer + T * (c - 1))] if not (isinstance(c, int) and c < 2) else []))
                for u in range(T):
                    s = h * T + u
                    pool.indirect_dma_start(msg[:, s, :], None, source,
                                            bass.IndirectOffsetOnAxis(cring[:, s:s + 1], 0)).then_inc(s_g[s], 16)

            for layer, source in enumerate((emb, table1)):
                if layer:
                    pool.wait_ge(s_t1w, 16 * (NB // GRP))
                for c in range(2):
                    gather_step(layer, source, c, c)
                with pool.Fori(1, NST // 2) as i:
                    for h in range(2):
                        gather_step(layer, source, 2 * i + h, h)

            pool.wait_ge(s_cw, 16 * (NB // GRP))
            pool.wait_ge(s_sid, 1)
            for bt in range(BT):
                half = bt % 2
                if bt >= 2:
                    pool.wait_ge(s_ss, bt - 1)
                for l in range(L):
                    pool.indirect_dma_start(seq[:, half, l, :], None, combined,
                                            bass.IndirectOffsetOnAxis(sidi[:, l, bt:bt + 1], 0)
                                            ).then_inc(s_sq[half * NG + l // LG], 16)

        @block.scalar
        def _(act):
            for dst, src in ((it_i, items), (al_i, alias), (in_i, inputs)):
                act.dma_start(dst[:, :, :], src.rearrange("(b p) l -> p b l", p=P)).then_inc(s_sess, 16)
            act.dma_start(w1a[:, :], w_1[0:D, :]).then_inc(s_wts, 16)
            act.dma_start(w1b[:, :], w_1[D:2 * D, :]).then_inc(s_wts, 16)
            act.dma_start(w2c[:, :], w_2).then_inc(s_wts, 16)
            act.dma_start(g1[:, :], glu1_w).then_inc(s_wts, 16)
            act.dma_start(g2[:, :], glu2_w).then_inc(s_wts, 16)
            act.dma_start(b1c[:, :], glu1_b.rearrange("(p o) -> p o", o=1)).then_inc(s_wts, 16)
            act.dma_start(erow[:, :], emb[0:L, :]).then_inc(s_wts, 16)
            for n in range(NB // 2):
                act.wait_ge(s_eqm, n + 1)
                ge(act, s_eqs, n)
                act.activation(eqk, eqm, ACT.Copy, accum_out=counts[:, 2 * n + 1:2 * n + 2]).then_inc(s_eqs, 1)
            act.wait_ge(s_wT, 3)
            act.copy(g1T[:, :], bank[5][:, 0:D]).then_inc(s_wTc, 1)
            act.copy(g2T[:, :], bank[5][:, D:2 * D]).then_inc(s_wTc, 1)
            act.copy(eT[:, :], bank[5][:, 2 * D:2 * D + L]).then_inc(s_wTc, 1)
            act.wait_ge(s_pos, 1)
            act.copy(posb[:, :], bank[6][:, 0:L]).then_inc(s_posc, 1)
            for g in range(0, NB, 2):
                act.wait_ge(s_t1, g + 1)
                act.copy(big[:, 2 * D * g:2 * D * (g + 1)], bank[5][:, 0:2 * D]).then_inc(s_t1a, 1)
            for g in range(NB):
                act.wait_ge(s_g2r, g + 1)
                for q in range(2):
                    ge(act, s_ssq, 2 * g + q - 1)
                    act.activation(sqj[:, q, :], acc[:, (2 * g + q) * D:(2 * g + q + 1) * D], ACT.Square,
                                   scale=1.0 / (LAYERS + 1), accum_out=ssq[:, 2 * g + q:2 * g + q + 1]).then_inc(s_ssq, 1)
            act.wait_ge(s_ssq, 2 * NB)
            act.activation(ginv[:, :], ssq[:, :], ACT.Sqrt).then_inc(s_nrm, 1)
            act.wait_ge(s_gi, 3)
            for g in range(NB):
                ge(act, s_gnT, g - 1)
                for q in range(2):
                    last = act.activation(gnr[:, g % 2, q, :], acc[:, (2 * g + q) * D:(2 * g + q + 1) * D], ACT.Copy,
                                          scale=ginv2[:, 2 * g + q:2 * g + q + 1])
                last.then_inc(s_gn, 1)
            for bt in range(BT):
                for k in range(NG):
                    m, w = NG * bt + k, min(LG, L - LG * k)
                    act.wait_ge(s_x, m + 1)
                    ge(act, s_z, m - 1)
                    act.copy(xT[:, m % 2, 0:w * P], bank[m % 2][:, 0:w * P]).then_inc(s_xc, 1)
                    act.wait_ge(s_z, m + 1)
                    if k == 0 and bt:
                        act.wait_ge(s_y, NG * bt)
                    for j in range(w):
                        l = LG * k + j
                        last = act.activation(nh1[:, l * P:(l + 1) * P], bank[2 + m % 2][:, j * P:(j + 1) * P],
                                              ACT.Tanh, bias=posb[:, L - 1 - l:L - l])
                    last.then_inc(s_th, 1)
                act.wait_ge(s_x, NG * (bt + 1))
                act.copy(hsT[:, :], bank[4][:, 0:P]).then_inc(s_hsc, 1)
                for k in range(NG):
                    m, w = NG * bt + k, min(LG, L - LG * k)
                    act.wait_ge(s_ya, m + 1)
                    if m >= 2:
                        act.wait_ge(s_bt, m - 1)
                    act.activation(nh2[:, m % 2, 0:w * P], ysum[:, m % 2, 0:w * P], ACT.Sigmoid).then_inc(s_sg, 1)
                act.wait_ge(s_sn, 5 * bt + 1)
                act.activation(rown[:, 1:2], rown[:, 0:1], ACT.Sqrt).then_inc(s_sn, 1)
                for n in range(0, NS, 2):
                    m = (-(-NS // 2)) * bt + n // 2
                    w = 512 if n < NS - 1 else REM
                    act.wait_ge(s_sc, NS * bt + n + 1)
                    if m >= 4:
                        act.wait_ge(s_out[m % 4], 16 * (m // 4))
                    act.copy(ostage[:, m % 4, 0:w], bank[5][:, 0:w]).then_inc(s_sca, 1)

        @block.vector
        def _(dve):
            dve.memset(e_row[:, COLS:ECOLS], -1).then_inc(s_init, 1)
            dve.memset(e_col[:, COLS:ECOLS], 0).then_inc(s_init, 1)
            dve.memset(e_val[:, COLS:ECOLS], 0.0).then_inc(s_init, 1)
            dve.memset(pay[:, :, 3:4], 0.0).then_inc(s_init, 1)
            chain = [0]

            def link(ins):
                chain[0] += 1
                ins.then_inc(s_v, 1)
                dve.wait_ge(s_v, chain[0])

            dve.wait_ge(s_edge, 96)
            dve.wait_ge(s_init, 4)
            link(dve.tensor_single_scalar(bkt_i, e_row, BUCKET.bit_length() - 1, ALU.arith_shift_right))
            link(dve.tensor_copy(bkt, bkt_i))
            for b in range(NB):
                if b % 2:
                    ge(dve, s_eqs, b // 2)
                    dve.tensor_scalar(eqm, bkt, float(b), None, ALU.is_equal).then_inc(s_eqm, 1)
                else:
                    ge(dve, s_cntv, b // 2)
                    dve.tensor_scalar(eqj, bkt, float(b), 0.0, ALU.is_equal, ALU.add,
                                      accum_out=counts[:, b:b + 1]).then_inc(s_cntv, 1)
            link(dve.tensor_single_scalar(bkt_i, e_row, BUCKET - 1, ALU.bitwise_and))
            dve.tensor_copy(pay[:, :, 0:1], bkt_i.unsqueeze(2)).then_inc(s_bkt, 1)
            dve.tensor_scalar(pay[:, :, 1:2], e_col.unsqueeze(2), 0.0, float(N - 1), ALU.max, ALU.min).then_inc(s_bkt, 1)
            dve.tensor_copy(pay[:, :, 2:3], e_val.unsqueeze(2)).then_inc(s_bkt, 1)
            dve.wait_ge(s_tot, 1)
            link(dve.tensor_scalar(toti[:, :], bank[4][:, 0:NB], float(P - 1), None, ALU.add))
            link(dve.tensor_single_scalar(toti2[:, :], toti[:, :], P.bit_length() - 1, ALU.arith_shift_right))
            link(dve.tensor_copy(ntile[:, :], toti2[:, :]))
            dve.wait_ge(s_cst, 12)
            link(dve.tensor_tensor_scan(cum[:, :], ones[:, 0:NB], ntile[:, :], 0.0, ALU.mult, ALU.add))
            link(dve.tensor_tensor(start[:, :], cum[:, :], ntile[:, :], ALU.subtract))
            link(dve.tensor_scalar(base[:, 0, :], start[:, :], float(P), None, ALU.mult))
            link(dve.tensor_tensor_reduce(junkb[0:NB, :], start[0:NB, :], ident[0:NB, 0:NB], 1.0, 0.0,
                                          ALU.mult, ALU.add, startc[0:NB, :]))
            dve.tensor_scalar(tile_ge[0:NB, :], tile_iota[0:NB, :], startc[0:NB, 0:1], None, ALU.is_ge).then_inc(s_tge, 1)
            dve.wait_ge(s_tge, 2)
            for n in range(3):
                a, b = n * TW, min(NT, (n + 1) * TW)
                dve.tensor_scalar(tile_off[0:1, a:b], bank[5 + n][0:1, 0:b - a], -1.0, float(BUCKET),
                                  ALU.add, ALU.mult).then_inc(s_toff, 1)
            dve.wait_ge(s_sess, 48)
            dve.tensor_copy(al_f[:, :, :], al_i[:, :, :])
            link(dve.tensor_copy(it_f[:, :, :], it_i[:, :, :]))
            link(dve.tensor_scalar(it_n[:, :, :], it_f[:, :, :], 0.0, float(N), ALU.is_lt, ALU.mult))
            link(dve.tensor_tensor(it_f[:, :, :], it_f[:, :, :], it_n[:, :, :], ALU.add))
            link(dve.tensor_scalar(it_n[:, :, :], it_f[:, :, :], 0.0, float(N - 1), ALU.max, ALU.min))
            link(dve.tensor_scalar(mask[:, :, :], in_i[:, :, :], 0.0, None, ALU.not_equal))
            link(dve.tensor_reduce(mcnt[:, :], mask[:, :, :], AX_X, ALU.add))
            link(dve.reciprocal(mrec[:, :], mcnt[:, :]))
            for bt in range(BT):
                link(dve.tensor_scalar(maskn[:, bt, :], mask[:, bt, :], mrec[:, bt:bt + 1], None, ALU.mult))

            def build(c, h):
                dve.tensor_tensor(oh[:, h, :, :], iota_bc[:, :, :],
                                  bkt[:, bass.ds(c * C, C)].unsqueeze(1).broadcast_to([P, NB, C]),
                                  ALU.is_equal).then_inc(s_oh, 1)

            def place(c, it, h, v0):
                dve.wait_ge(s_rank, c + 1)
                dve.tensor_tensor(rank[:, :, :], octv(h), base[:, h, :].unsqueeze(2).broadcast_to([P, NB, C]),
                                  ALU.add).then_inc(s_rel, 1)
                dve.tensor_tensor(base[:, 1 - h, :], base[:, h, :], bank[2 + h][:, 0:NB], ALU.add).then_inc(s_rel, 1)
                dve.wait_ge(s_rel, 2 * c + 2)
                dve.tensor_tensor(rank[:, :, :], rank[:, :, :], oh[:, h, :, :], ALU.mult).then_inc(s_v, 1)
                dve.wait_ge(s_v, v0 + 1)
                dve.tensor_reduce(posf[:, :], rank[:, :, :].rearrange("p b t -> p t b"), AX_X, ALU.add).then_inc(s_v, 1)
                dve.wait_ge(s_v, v0 + 2)
                dve.tensor_copy(posi[:, :], posf[:, :]).then_inc(s_v, 1)
                dve.wait_ge(s_v, v0 + 3)
                dve.tensor_single_scalar(pos_p[:, :], posi[:, :], P - 1, ALU.bitwise_and)
                dve.tensor_single_scalar(pos_j[:, :], posi[:, :], P.bit_length() - 1,
                                         ALU.arith_shift_right).then_inc(s_v, 1)
                dve.wait_ge(s_v, v0 + 4)
                ge(dve, s_sct[h], 16 * C * it)
                dve.scalar_tensor_tensor(slot_i[:, h, :], pos_p[:, :], float(NT), pos_j[:, :], ALU.mult, ALU.add)
                dve.tensor_copy(pring[:, h, :].rearrange("p (t w) -> p t w", w=4),
                                pay[:, bass.ds(c * C, C), :]).then_inc(s_slot, 1)

            def session_rows(l):
                for bt in range(BT):
                    dve.scalar_tensor_tensor(junkl[:, bt, :], iota_l[:, :], al_f[:, bt, bass.ds(l, 1)], it_n[:, bt, :],
                                             ALU.is_equal, ALU.mult, accum_out=sidf[:, bass.ds(l, 1), bt])

            def sort_pair(it, v):
                for h in range(2):
                    build(2 * it + h + 1, 1 - h)
                    place(2 * it + h, it, h, v + 4 * h)

            dve.wait_ge(s_bkt, 3)
            build(0, 0)
            v0 = chain[0]
            sort_pair(0, v0)
            with dve.Fori(1, L + 1) as i:
                sort_pair(i, v0 + 8 * i)
                session_rows(i - 1)
            with dve.Fori(L + 1, NCH // 2) as i:
                sort_pair(i, v0 + 8 * i)
            place(NCH - 1, NCH // 2, 0, v0 + 4 * (NCH - 1))
            chain[0] = v0 + 4 * NCH
            dve.tensor_copy(sidi[:, :, :], sidf[:, :, :]).then_inc(s_sid, 1)

            def fetch(c, h, layer):
                dve.tensor_copy(mring[:, h * T * 4:(h + 1) * T * 4], meta[:, bass.ds(c * T * 4, T * 4)])
                dve.tensor_copy(cring[:, h * T:(h + 1) * T].unsqueeze(2),
                                meta[:, bass.ds(c * T * 4, T * 4)].rearrange("p (t w) -> p t w", w=4)[:, :, 1:2]
                                ).then_inc(s_mr, 1)

            def round_step(layer, c, h, first=False, last=False):
                for u in range(T):
                    if not first:
                        dve.wait_ge(s_mm, NT * layer + T * (c - 1) + u + 1)
                    if not last:
                        if u == 0:
                            dve.wait_ge(s_mr, NST * layer + c + 1)
                        o = (h * T + u) * 4
                        dve.tensor_scalar(onehot[:, u % SR, :], iota_r[:, :], mring[:, o:o + 1], mring[:, o + 2:o + 3],
                                          ALU.is_equal, ALU.mult).then_inc(s_S, 1)
                    if not first:
                        off = dve.value_load(tile_off[0:1, bass.ds(T * (c - 1) + u, 1)], min_val=0,
                                             max_val=ROWS - BUCKET)
                        ge(dve, s_acc, NT * layer + T * (c - 1) + u + 1)
                        dve.tensor_tensor(acc[:, bass.ds(off, BUCKET)], acc[:, bass.ds(off, BUCKET)],
                                          bank[u % PR][:, 0:BUCKET], ALU.add).then_inc(s_acc, 1)

            dve.memset(rown0[:, :], 0.0).then_inc(s_acc, 1)
            dve.wait_ge(s_meta, 16)
            dve.wait_ge(s_toff, 3)
            dve.wait_ge(s_zero, 16)
            for layer in range(LAYERS):
                if layer:
                    dve.wait_ge(s_mm, NT)
                fetch(0, 0, layer)
                round_step(layer, 0, 0, first=True)
                fetch(1, 1, layer)
                with dve.Fori(0, NST // 2 - 1) as i:
                    for h in range(2):
                        round_step(layer, 2 * i + h + 1, 1 - h)
                        fetch(2 * i + h + 2, h, layer)
                round_step(layer, NST - 1, 1)
                round_step(layer, NST, 0, last=True)
                if layer == 0:
                    for g in range(1, NB, 2):
                        dve.wait_ge(s_t1, g + 1)
                        dve.tensor_copy(big[:, 2 * D * g:2 * D * (g + 1)], bank[6][:, 0:2 * D]).then_inc(s_t1v, 1)
                    dve.wait_ge(s_t1w, 16 * (NB // GRP))
                    dve.memset(big_rows[:, emb_full, :], 0.0).then_inc(s_fz, 1)
            dve.memset(feat_rows[:, emb_full, :], 0.0).then_inc(s_fz, 1)

            dve.wait_ge(s_eld, 32)
            for g in range(NB):
                cols = slice(2 * D * g, 2 * D * (g + 1))
                dve.wait_ge(s_t2, g + 1)
                dve.tensor_tensor(acc[:, cols], bank[5 + g % 2][:, 0:2 * D], big[:, cols], ALU.add).then_inc(s_g2r, 1)
                dve.wait_ge(s_g2r, g + 1)
                if g == 0:
                    dve.wait_ge(s_fld, 32)
                dve.scalar_tensor_tensor(big[:, cols], acc[:, cols], 1.0 / (LAYERS + 1), ring[:, cols],
                                         ALU.mult, ALU.add).then_inc(s_cmb, 1)
            dve.wait_ge(s_nrm, 1)
            dve.tensor_scalar(ginv[:, :], ginv[:, :], EPS, None, ALU.max).then_inc(s_gi, 1)
            dve.wait_ge(s_gi, 1)
            dve.reciprocal(ginv[:, :], ginv[:, :]).then_inc(s_gi, 1)
            dve.wait_ge(s_gi, 2)
            dve.tensor_scalar(ginv2[:, :], ginv[:, :], 1.0 / (LAYERS + 1), None, ALU.mult).then_inc(s_gi, 1)
            for g in range(NB):
                dve.wait_ge(s_gnT, g + 1)
                dve.tensor_copy(acc[:, 2 * D * g:2 * D * (g + 1)], bank[5 + g % 2][:, 0:2 * D]).then_inc(s_gnc, 1)
            dve.wait_ge(s_cw, 16 * (NB // GRP))
            for bt in range(BT):
                half = bt % 2
                for k in range(NG):
                    m, w = NG * bt + k, min(LG, L - LG * k)
                    if m >= 2:
                        dve.wait_ge(s_x, m - 1)
                    for j in range(w):
                        last = dve.tensor_scalar(dmask[:, m % 2, j, :], ident[:, :],
                                                 maskn[:, bt, LG * k + j:LG * k + j + 1], None, ALU.mult)
                    last.then_inc(s_dm, 1)
                dve.wait_ge(s_p2, bt + 1)
                dve.tensor_scalar(bias2[:, :], bank[7][:, 0:P], b1c[:, 0:1], None, ALU.add).then_inc(s_b2, 1)
                dve.wait_ge(s_b2, bt + 1)
                for k in range(NG):
                    m, w = NG * bt + k, min(LG, L - LG * k)
                    dve.wait_ge(s_y, m + 1)
                    if m >= 2:
                        dve.wait_ge(s_sg, m - 1)
                    dve.tensor_tensor(ysum[:, m % 2, 0:w * P].rearrange("p (l n) -> p l n", n=P),
                                      bank[5 + m % 2][:, 0:w * P].rearrange("p (l n) -> p l n", n=P),
                                      bias2[:, :].unsqueeze(1).broadcast_to([P, w, P]), ALU.add).then_inc(s_ya, 1)
                dve.wait_ge(s_bt, NG * (bt + 1))
                dve.tensor_tensor(beta[:, :], bank[7][:, 256:256 + L], mask[:, bt, :], ALU.mult).then_inc(s_bm, 1)
                dve.wait_ge(s_bm, bt + 1)
                for l in range(L):
                    if l >= 2:
                        dve.wait_ge(s_v, chain[0] + l - 1)
                        dve.scalar_tensor_tensor(sess[:, l % 4, :], seq[:, half, l, :], beta[:, l:l + 1],
                                                 sess[:, (l - 2) % 4, :], ALU.mult, ALU.add).then_inc(s_v, 1)
                    else:
                        dve.tensor_scalar(sess[:, l, :], seq[:, half, l, :], beta[:, l:l + 1], None,
                                          ALU.mult).then_inc(s_v, 1)
                chain[0] += L
                dve.wait_ge(s_v, chain[0])
                dve.tensor_tensor(junk[:, :], sess[:, (L - 1) % 4, :], sess[:, (L - 2) % 4, :], ALU.add).then_inc(s_ss, 1)
                dve.wait_ge(s_ss, bt + 1)
                dve.tensor_tensor_reduce(sess[:, 0, :], junk[:, :], junk[:, :], 1.0, 0.0, ALU.mult, ALU.add,
                                         rown[:, 0:1]).then_inc(s_sn, 1)
                dve.wait_ge(s_sn, 5 * bt + 2)
                dve.tensor_scalar(rown[:, 2:3], rown[:, 1:2], EPS, None, ALU.max).then_inc(s_sn, 1)
                dve.wait_ge(s_sn, 5 * bt + 3)
                dve.reciprocal(rown[:, 3:4], rown[:, 2:3]).then_inc(s_sn, 1)
                dve.wait_ge(s_sn, 5 * bt + 4)
                dve.tensor_scalar(sess[:, 1, :], junk[:, :], rown[:, 3:4], W_K, ALU.mult, ALU.mult).then_inc(s_sn, 1)
                dve.wait_ge(s_sT, bt + 1)
                dve.tensor_copy(selT[:, :], bank[7][:, 384:384 + P]).then_inc(s_sTc, 1)
                for n in range(1, NS, 2):
                    m = (-(-NS // 2)) * bt + n // 2
                    dve.wait_ge(s_sc, NS * bt + n + 1)
                    if m >= 4:
                        dve.wait_ge(s_out[m % 4], 16 * (m // 4))
                    dve.tensor_copy(ostage[:, m % 4, 512:1024], bank[6][:, :]).then_inc(s_scv, 1)

        @block.tensor
        def _(pe):
            pe.wait_ge(s_wts, 112)
            pe.wait_ge(s_cst, 12)
            pe.transpose(bank[5][:, 0:D], g1[:, :], ident[:, :]).then_inc(s_wT, 1)
            pe.transpose(bank[5][:, D:2 * D], g2[:, :], ident[:, :]).then_inc(s_wT, 1)
            pe.transpose(bank[5][:, 2 * D:2 * D + L], erow[:, :], ident[0:L, 0:L]).then_inc(s_wT, 1)
            pe.wait_ge(s_cntv, (NB + 1) // 2)
            pe.wait_ge(s_eqs, NB // 2)
            pe.matmul(bank[4][:, 0:NB], ones[:, :], counts[:, :], start=True, stop=True).then_inc(s_tot, 1)
            pe.wait_ge(s_wTc, 3)
            pe.matmul(bank[6][:, 0:L], w1a[:, :], eT[:, :], start=True, stop=True).then_inc(s_pos, 1)
            pe.wait_ge(s_posc, 1)
            pe.wait_ge(s_tge, 1)
            for n in range(3):
                a, b = n * TW, min(NT, (n + 1) * TW)
                last = pe.matmul(bank[5 + n][0:1, 0:b - a], onesb[0:NB, 0:1], tile_ge[0:NB, a:b], start=True, stop=True)
            last.then_inc(s_tge, 1)

            def rank_step(c, h):
                pe.wait_ge(s_oh, c + 1)
                ge(pe, s_rel, 2 * (c - 1))
                pe.matmul(octv(h), lower[:, :], oh[:, h, :, :], start=True, stop=False, skip_group_check=True)
                for k in range(1, C):
                    pe.matmul(octv(h)[:, :, k:C], onesb[:, :], oh[:, h, :, 0:C - k], start=False, stop=(k == C - 1),
                              skip_group_check=True)
                for t in range(C):
                    last = pe.matmul(bank[2 + h][:, 0:NB], onesb[:, :], oh[:, h, :, t], start=(t == 0), stop=(t == C - 1))
                last.then_inc(s_rank, 1)

            for c in range(2):
                rank_step(c, c)
            with pe.Fori(1, NCH // 2) as i:
                for h in range(2):
                    rank_step(2 * i + h, h)
            rank_step(NCH - 1, 0)

            def products(layer, c, it, h):
                for u in range(T):
                    j = NT * layer + T * c + u
                    pe.wait_ge(s_g[h * T + u], 16 * ((NST // 2) * layer + it + 1))
                    pe.wait_ge(s_S, j + 1)
                    ge(pe, s_acc, j + 2 - PR)
                    pe.matmul(bank[u % PR][:, 0:BUCKET], msg[:, h * T + u, :], onehot[:, u % SR, :],
                              start=True, stop=True).then_inc(s_mm, 1)

            for layer in range(LAYERS):
                for c in range(2):
                    products(layer, c, 0, c)
                with pe.Fori(1, NST // 2) as i:
                    for h in range(2):
                        products(layer, 2 * i + h, i, h)
                pe.wait_ge(s_acc, NT * (layer + 1) + 1)
                for g in range(NB):
                    if layer == 0:
                        ge(pe, (s_t1a, s_t1v)[g % 2], g // 2)
                    else:
                        ge(pe, s_g2r, g - 1)
                    for q in range(2):
                        last = pe.transpose(bank[5 + g % 2][:, q * D:(q + 1) * D],
                                            acc[:, (2 * g + q) * D:(2 * g + q + 1) * D], ident[:, :])
                    last.then_inc((s_t1, s_t2)[layer], 1)
            for g in range(NB):
                pe.wait_ge(s_gn, g + 1)
                if g < 2:
                    pe.wait_ge(s_g2r, NB)
                ge(pe, s_gnc, g - 1)
                for q in range(2):
                    last = pe.transpose(bank[5 + g % 2][:, q * D:(q + 1) * D], gnr[:, g % 2, q, :], ident[:, :])
                last.then_inc(s_gnT, 1)

            for bt in range(BT):
                half = bt % 2

                def first_product(k):
                    m, w = NG * bt + k, min(LG, L - LG * k)
                    pe.wait_ge(s_xc, m + 1)
                    ge(pe, s_th, m - 1)
                    pe.matmul(bank[2 + m % 2][:, 0:w * P], w1b[:, :], xT[:, m % 2, 0:w * P],
                              start=True, stop=True).then_inc(s_z, 1)

                for k in range(NG):
                    m, w = NG * bt + k, min(LG, L - LG * k)
                    pe.wait_ge(s_sq[half * NG + k], 16 * w * (bt // 2 + 1))
                    pe.wait_ge(s_dm, m + 1)
                    ge(pe, s_xc, m - 1)
                    if k == 0 and bt:
                        pe.wait_ge(s_hsc, bt)
                    for j in range(w):
                        l = LG * k + j
                        pe.matmul(bank[4][:, 0:P], seq[:, half, l, :], dmask[:, m % 2, j, :],
                                  start=(l == 0), stop=(l == L - 1))
                    for j in range(w):
                        last = pe.transpose(bank[m % 2][:, j * P:(j + 1) * P], seq[:, half, LG * k + j, :], ident[:, :])
                    last.then_inc(s_x, 1)
                    if k:
                        first_product(k - 1)
                first_product(NG - 1)
                pe.wait_ge(s_hsc, bt + 1)
                if bt:
                    pe.wait_ge(s_sTc, bt)
                pe.matmul(bank[7][:, 0:P], g2T[:, :], hsT[:, :], start=True, stop=True).then_inc(s_p2, 1)

                def read_out(k):
                    m, w = NG * bt + k, min(LG, L - LG * k)
                    pe.wait_ge(s_sg, m + 1)
                    if k == 0:
                        pe.wait_ge(s_b2, bt + 1)
                        if bt:
                            pe.wait_ge(s_bm, bt)
                    for j in range(w):
                        l = LG * k + j
                        last = pe.matmul(bank[7][:, 256 + l:257 + l], nh2[:, m % 2, j * P:(j + 1) * P], w2c[:, :],
                                         start=True, stop=True)
                    last.then_inc(s_bt, 1)

                for k in range(NG):
                    m, w = NG * bt + k, min(LG, L - LG * k)
                    pe.wait_ge(s_th, m + 1)
                    ge(pe, s_ya, m - 1)
                    if k < 2:
                        pe.wait_ge(s_gnc, NB)
                        if bt:
                            pe.wait_ge(s_sca, (-(-NS // 2)) * bt)
                            pe.wait_ge(s_scv, (NS // 2) * bt)
                    pe.matmul(bank[5 + m % 2][:, 0:w * P], g1T[:, :], nh1[:, k * LG * P:(k * LG + w) * P],
                              start=True, stop=True).then_inc(s_y, 1)
                    if k:
                        read_out(k - 1)
                read_out(NG - 1)
                pe.wait_ge(s_sn, 5 * (bt + 1))
                pe.transpose(bank[7][:, 384:384 + P], sess[:, 1, :], ident[:, :]).then_inc(s_sT, 1)
                pe.wait_ge(s_sTc, bt + 1)
                for n in range(NS):
                    w = 512 if n < NS - 1 else REM
                    if n < 2:
                        pe.wait_ge(s_ya, NG * (bt + 1))
                    elif n % 2:
                        pe.wait_ge(s_scv, (NS // 2) * bt + n // 2)
                    else:
                        pe.wait_ge(s_sca, (-(-NS // 2)) * bt + n // 2)
                    pe.matmul(bank[5 + n % 2][:, 0:w], selT[:, :], acc[:, 512 * n:512 * n + w],
                              start=True, stop=True).then_inc(s_sc, 1)


_INS = ["r_items", "r_inputs", "r_alias_inputs", "L0_rec_item_features", "L0_rec_adj_row", "L0_rec_adj_col",
        "L0_rec_adj_val", "L0_rec_emb", "L0_rec_w_1", "L0_rec_w_2", "L0_rec_glu1_w", "L0_rec_glu1_b", "L0_rec_glu2_w"]


def kernel(**inputs):
    import numpy as _np
    import concourse.bacc as _bacc
    from concourse import mybir as _mybir
    from concourse.bass_utils import run_bass_kernel_spmd as _run

    nc = _bacc.Bacc("TRN2", target_bir_lowering=False, num_devices=1)
    arrays, args = {}, []
    for name in _INS:
        a = _np.ascontiguousarray(inputs[name])
        arrays[f"in_{name}"] = a
        args.append(nc.dram_tensor(f"in_{name}", a.shape, _mybir.dt.from_np(a.dtype), kind="ExternalInput").ap())
    shape = (inputs["r_items"].shape[0], inputs["L0_rec_emb"].shape[0])
    args.append(nc.dram_tensor("scores", shape, _mybir.dt.float32, kind="ExternalOutput").ap())
    recommender_program(nc, *args)
    r = _run(nc, [arrays], core_ids=[0])
    return r.results[0]["scores"]
```

```python
from contextlib import ExitStack

import concourse.bass as bass
from concourse import mybir

ALU = mybir.AluOpType
ACT = mybir.ActivationFunctionType
AX_X = mybir.AxisListType.X
F32 = mybir.dt.float32
BF16 = mybir.dt.bfloat16
I32 = mybir.dt.int32

P = 128
W_K = 12.0
EPS = 1e-12
LAYERS = 2


def ge(eng, sem, value):
    if isinstance(value, int) and value <= 0:
        return
    eng.wait_ge(sem, value)


def recommender_program(nc, items, inputs, alias, features, adj_row, adj_col, adj_val, emb,
                        w_1, w_2, glu1_w, glu1_b, glu2_w, out):
    B, L = items.shape
    N, D = emb.shape
    E = adj_row.shape[0]
    BT = B // P
    BUCKET = 256
    NB = -(-N // BUCKET)
    ROWS = NB * BUCKET
    COLS = E // P
    TAIL = E - COLS * P
    C = 8
    SG = 10
    GR = -(-(COLS + 1) // (C * SG))
    R = 4
    NK = -(-(SG * C * P + NB * (R - 1)) // (R * P))
    LC = NK * R
    ECOLS = (GR * SG + 2) * C
    T = 20
    NT = -(-((E + GR * NB * (R - 1) + NB * (P - 1)) // P) // T) * T
    NST = NT // T
    FAR = float(2 ** 20)
    SR, PR = 10, 5
    assert NST % 2 == 0 and SG % 2 == 0 and D == P and 0 < TAIL < P and T % SR == 0 and SR % PR == 0
    LG = 4
    NG = -(-L // LG)
    NS = -(-N // 512)
    REM = N - (NS - 1) * 512
    TW = -(-NT // 3)

    with ExitStack() as ctx:
        def sb(name, shape, dt=F32):
            return ctx.enter_context(nc.sbuf_tensor(name, shape, dt))

        def sem(name):
            return ctx.enter_context(nc.semaphore(name))

        slots = nc.dram_tensor("sorted_edges", [NT * P // R, 2 * R], F32).ap()
        table1 = nc.dram_tensor("table1", [ROWS, D], F32).ap()
        combined = nc.dram_tensor("combined", [ROWS, D], F32).ap()

        acc = sb("acc", [P, ROWS])
        big = sb("big", [P, ROWS])
        ring = sb("ring", [P, 2 * L * D])
        at = [0]

        def carve(base, words, dt=F32):
            v = base[:, at[0]:at[0] + words]
            at[0] += words
            return v if dt == F32 else v.bitcast(dt)

        e_row = carve(big, ECOLS, I32)
        e_col = carve(big, ECOLS, I32)
        e_val = carve(big, ECOLS)
        bkt_i = carve(big, ECOLS, I32)
        bkt = carve(big, ECOLS // 2, BF16)
        col_f = carve(big, ECOLS)
        code = carve(big, ECOLS)
        block_at = carve(big, NK * P)
        iota_c = carve(big, LC * C // 2, BF16).rearrange("p (c t) -> p c t", t=C)
        hot_c = carve(big, LC * C, BF16).rearrange("p (h c t) -> p h c t", h=2, t=C)
        assert at[0] <= ROWS
        at[0] = 0
        tile_iota = carve(ring, NT)
        tile_ge = carve(ring, NT // 2, BF16)
        at_p = carve(ring, 2 * C * P).rearrange("p (h t n) -> p h t n", h=2, t=C)
        at_c = carve(ring, 2 * C * 2 * LC).rearrange("p (h t w n) -> p h t w n", h=2, t=C, w=2)
        begun = carve(ring, NK * P)
        gofs = carve(ring, GR * NB).rearrange("p (g b) -> p g b", g=GR)
        delta = carve(ring, GR * (NB + 1)).rearrange("p (g b) -> p g b", g=GR)
        dstep = carve(ring, GR * (NB + 1)).rearrange("p (g b) -> p g b", g=GR)
        rank = carve(ring, NB * C).rearrange("p (b t) -> p b t", t=C)
        assert at[0] <= 2 * L * D
        sorted_rows = big[:, 0:-(-NT // P) * 2 * P].rearrange("p (m s w) -> p m s w", w=2, s=P)
        at[0] = 0
        m_code = carve(ring, NT, I32)
        m_lo = carve(ring, NT)
        m_val = carve(ring, NT)
        m_col = carve(ring, NT, I32)
        msg = carve(ring, 2 * T * D).rearrange("p (s d) -> p s d", d=D)
        onehot = carve(ring, SR * BUCKET).rearrange("p (s r) -> p s r", r=BUCKET)
        assert at[0] <= 2 * L * D
        at[0] = 0
        nh1 = carve(big, L * P)
        xT = carve(big, 2 * LG * P).rearrange("p (s n) -> p s n", s=2)
        ysum = carve(big, 2 * LG * P).rearrange("p (s n) -> p s n", s=2)
        nh2 = carve(big, 2 * LG * P).rearrange("p (s n) -> p s n", s=2)
        hsum = carve(big, 4 * D).rearrange("p (s d) -> p s d", s=4)
        hrow = carve(big, D)
        hsT = carve(big, P)
        bias2 = carve(big, P)
        beta = carve(big, L)
        sess = carve(big, 4 * D).rearrange("p (s d) -> p s d", s=4)
        selT = carve(big, P)
        junk = carve(big, D)
        rown = carve(big, 8)
        assert at[0] <= ROWS
        seq = ring[:, :].rearrange("p (h l d) -> p h l d", h=2, l=L)

        stage = sb("stage", [P, 4 * 512 * 2])
        ostage = stage[:, :].rearrange("p (s n) -> p s n", s=4)
        gnr = sb("gnr", [P, 2, 2, D])
        ident = sb("ident", [P, P])
        ones = sb("ones", [P, P])
        onesb = sb("onesb", [P, P], BF16)
        lower = sb("lower", [P, P], BF16)
        iota_r = sb("iota_r", [P, BUCKET])
        iota_bc = sb("iota_bc", [P, NB, C], BF16)
        iota_l = sb("iota_l", [P, L])
        gate = sb("gate", [P, 3])
        toti = sb("toti", [P, NB], I32)
        toti2 = sb("toti2", [P, NB], I32)
        sqj = sb("sqj", [P, 2, D])
        prime = sb("prime", [P, 1])
        tot = sb("tot", [P, NB])
        gcnt_now = sb("gcnt_now", [P, NB])
        ginv2 = sb("ginv2", [P, 2 * NB])
        ntile = sb("ntile", [P, NB])
        cum = sb("cum", [P, NB])
        start = sb("start", [P, NB])
        junkb = sb("junkb", [P, NB])
        at[0] = 0
        counts = [carve(stage, GR * NB, dt).rearrange("p (g b) -> p g b", b=NB) for dt in (F32, I32, I32, F32, F32)]
        gcnt, gpad_i, gpad_j, gpad, gcum = counts
        lstart = sb("lstart", [P, GR + 1, NB + 1])
        lscol = sb("lscol", [NB + 1, GR])
        dscol = sb("dscol", [NB + 1, GR])
        dsnow = sb("dsnow", [NB + 1, 1])
        block_id = sb("block_id", [P, NK])
        block_to = sb("block_to", [P, NK], I32)
        iota_p = sb("iota_p", [P, P], BF16)
        moved = sb("moved", [P, LC, 2])
        mlo = sb("mlo", [P, 2 * T])
        mval = sb("mval", [P, 2 * T])
        cring = sb("cring", [P, 2 * T], I32)
        startc = sb("startc", [P, 1])
        tile_off = sb("tile_off", [1, NT], I32)
        base = sb("base", [P, 2, NB])
        oh = sb("oh", [P, 2, NB, C], BF16)
        posf = sb("posf", [P, C])
        posi = sb("posi", [P, C], I32)
        place_i = sb("place_i", [P, 3, C], I32)
        place_p = sb("place_p", [P, 2, C], BF16)
        place_c = sb("place_c", [P, 2, C], BF16)
        idle = sb("idle", [P, 2])
        it_i = sb("it_i", [P, BT, L], I32)
        al_i = sb("al_i", [P, BT, L], I32)
        in_i = sb("in_i", [P, BT, L], I32)
        it_f = sb("it_f", [P, BT, L])
        it_n = sb("it_n", [P, BT, L])
        al_f = sb("al_f", [P, BT, L])
        mask = sb("mask", [P, BT, L])
        maskn = sb("maskn", [P, BT, L])
        mcnt = sb("mcnt", [P, BT])
        mrec = sb("mrec", [P, BT])
        sidf = sb("sidf", [P, L, BT])
        sidi = sb("sidi", [P, L, BT], I32)
        junkl = sb("junkl", [P, BT, L])
        ssq = sb("ssq", [P, 2 * NB])
        ginv = sb("ginv", [P, 2 * NB])
        w1a = sb("w1a", [D, D])
        w1b = sb("w1b", [D, D])
        w2c = sb("w2c", [D, 1])
        g1 = sb("g1", [D, D])
        g2 = sb("g2", [D, D])
        g1T = sb("g1T", [D, D])
        g2T = sb("g2T", [D, D])
        b1c = sb("b1c", [D, 1])
        erow = sb("erow", [L, D])
        eT = sb("eT", [D, L])
        posb = sb("posb", [D, L])

        bank = [ctx.enter_context(nc.psum_tensor(f"bank{i}", [P, 512], F32)) for i in range(8)]

        def octv(b):
            return bank[b][:, 0:NB * C].rearrange("p (b t) -> p b t", t=C)

        s_edge = sem("s_edge")
        s_sess = sem("s_sess")
        s_wts = sem("s_wts")
        s_cst = sem("s_cst")
        s_gate = sem("s_gate")
        s_init = sem("s_init")
        s_zero = sem("s_zero")
        s_v = sem("s_v")
        s_oh1 = sem("s_oh1")
        s_h = sem("s_h")
        s_red = sem("s_red")
        s_ls = sem("s_ls")
        s_lc = sem("s_lc")
        s_lcc = sem("s_lcc")
        s_tge = sem("s_tge")
        s_toff = sem("s_toff")
        s_oh = sem("s_oh")
        s_base = sem("s_base")
        s_rank = sem("s_rank")
        s_rel = sem("s_rel")
        s_tot = sem("s_tot")
        s_hc = sem("s_hc")
        s_hp = sem("s_hp")
        s_val = sem("s_val")
        s_pm = sem("s_pm")
        s_bg = sem("s_bg")
        s_dst = sem("s_dst")
        s_to = sem("s_to")
        s_gev = sem("s_gev")
        s_sct = sem("s_sct")
        s_free = sem("s_free")
        s_mtr = sem("s_mtr")
        s_mtc = sem("s_mtc")
        s_mta = sem("s_mta")
        s_meta = sem("s_meta")
        s_mr = sem("s_mr")
        s_g = [sem(f"s_g{u}") for u in range(2 * T)]
        s_S = sem("s_S")
        s_mm = sem("s_mm")
        s_acc = sem("s_acc")
        s_t1 = sem("s_t1")
        s_t1a = sem("s_t1a")
        s_t1v = sem("s_t1v")
        s_t1w = sem("s_t1w")
        s_eld = sem("s_eld")
        s_fld = sem("s_fld")
        s_fz = sem("s_fz")
        s_t2 = sem("s_t2")
        s_g2r = sem("s_g2r")
        s_ssq = sem("s_ssq")
        s_cmb = sem("s_cmb")
        s_cw = sem("s_cw")
        s_wT = sem("s_wT")
        s_wTc = sem("s_wTc")
        s_pos = sem("s_pos")
        s_posc = sem("s_posc")
        s_nrm = sem("s_nrm")
        s_gi = sem("s_gi")
        s_gn = sem("s_gn")
        s_gnT = sem("s_gnT")
        s_gnc = sem("s_gnc")
        s_sid = sem("s_sid")
        s_sq = [sem(f"s_sq{i}") for i in range(2 * NG)]
        s_x = sem("s_x")
        s_xc = sem("s_xc")
        s_hs = sem("s_hs")
        s_hT = sem("s_hT")
        s_z = sem("s_z")
        s_th = sem("s_th")
        s_hsc = sem("s_hsc")
        s_p2 = sem("s_p2")
        s_b2 = sem("s_b2")
        s_y = sem("s_y")
        s_ya = sem("s_ya")
        s_sg = sem("s_sg")
        s_bt = sem("s_bt")
        s_bm = sem("s_bm")
        s_ss = sem("s_ss")
        s_sn = sem("s_sn")
        s_sT = sem("s_sT")
        s_sTc = sem("s_sTc")
        s_sc = sem("s_sc")
        s_sca = sem("s_sca")
        s_scv = sem("s_scv")
        s_out = [sem(f"s_out{i}") for i in range(4)]

        block = ctx.enter_context(nc.Block())
        GRP = 7
        assert NB % GRP == 0
        emb_full = N // P
        emb_rest = N - emb_full * P
        tab = [t.rearrange("(g p) d -> p g d", p=P) for t in (table1, combined)]
        big_rows = big[:, :].rearrange("p (g d) -> p g d", d=D)
        acc_rows = acc[:, :].rearrange("p (g d) -> p g d", d=D)
        feat_rows = ring[:, 0:ROWS].rearrange("p (g d) -> p g d", d=D)

        @block.sync
        def _(sp):
            sp.wait_ge(s_init, 3)
            for n, (dst, src) in enumerate(((e_row, adj_row), (e_col, adj_col), (e_val, adj_val))):
                sp.dma_start(dst[:, 0:COLS], src[0:COLS * P].rearrange("(p t) -> p t", t=COLS)).then_inc(s_edge, 16)
                sp.dma_start(dst[0:TAIL, COLS:COLS + 1],
                             src[COLS * P:E].rearrange("(p t) -> p t", t=1)).then_inc(s_edge, 16)
            sp.wait_ge(s_cst, 1)
            sp.dma_start(slots.rearrange("(p x) w -> p (x w)", p=P), acc[:, 0:NT * 2]).then_inc(s_zero, 16)
            sp.wait_ge(s_free, GR + 2)
            lines = slots.rearrange("(j x) w -> j (x w)", x=P // R)
            full = NT // P
            sp.dma_start(big[:, 0:full * 2 * P].rearrange("p (m w) -> p m w", m=full),
                         lines[0:full * P, :].rearrange("(m p) w -> p m w", p=P)).then_inc(s_meta, 16)
            sp.dma_start(big[0:NT - full * P, full * 2 * P:(full + 1) * 2 * P], lines[full * P:NT, :]
                         ).then_inc(s_meta, 16)
            for r in range(NB // GRP):
                sp.wait_ge(s_t1a, (GRP * (r + 1) + 1) // 2)
                sp.wait_ge(s_t1v, (GRP * (r + 1)) // 2)
                a, b = 2 * GRP * r, 2 * GRP * (r + 1)
                sp.dma_start(tab[0][:, a:b, :], big_rows[:, a:b, :]).then_inc(s_t1w, 16)
            sp.wait_ge(s_t1w, 16 * (NB // GRP))
            sp.dma_start(big_rows[:, 0:emb_full, :],
                         emb[0:emb_full * P, :].rearrange("(g p) d -> p g d", p=P)).then_inc(s_eld, 16)
            sp.wait_ge(s_fz, 1)
            sp.dma_start(big_rows[0:emb_rest, emb_full, :], emb[emb_full * P:N, :]).then_inc(s_eld, 16)
            sp.wait_ge(s_fz, 2)
            sp.dma_start(feat_rows[0:emb_rest, emb_full, :], features[emb_full * P:N, :]).then_inc(s_fld, 16)
            sp.dma_start(feat_rows[:, 0:emb_full, :],
                         features[0:emb_full * P, :].rearrange("(g p) d -> p g d", p=P)).then_inc(s_fld, 16)
            for r in range(NB // GRP):
                sp.wait_ge(s_cmb, GRP * (r + 1))
                a, b = 2 * GRP * r, 2 * GRP * (r + 1)
                sp.dma_start(tab[1][:, a:b, :], big_rows[:, a:b, :]).then_inc(s_cw, 16)
            for bt in range(BT):
                for q in range(-(-NS // 2)):
                    m = (-(-NS // 2)) * bt + q
                    sp.wait_ge(s_sca, m + 1)
                    if 2 * q + 1 < NS:
                        sp.wait_ge(s_scv, (NS // 2) * bt + q + 1)
                    a, b = 1024 * q, min(1024 * q + 1024, N)
                    sp.dma_start(out[bt * P:(bt + 1) * P, a:b], ostage[:, m % 4, 0:b - a]).then_inc(s_out[m % 4], 16)
            total = (-(-NS // 2)) * BT
            for i in range(4):
                sp.wait_ge(s_out[i], 16 * ((total - i + 3) // 4))

        @block.gpsimd
        def _(pool):
            pool.memset(acc[:, :], 0.0).then_inc(s_cst, 1)
            pool.memset(gate[:, :], 0.0).then_inc(s_gate, 1)
            pool.memset(ones[:, :], 1.0).then_inc(s_cst, 1)
            pool.memset(ident[:, :], 0.0).then_inc(s_cst, 1)
            pool.memset(onesb[:, :], 1.0).then_inc(s_cst, 1)
            pool.iota(iota_r[:, :], [[1, BUCKET]], base=0, channel_multiplier=0,
                      allow_small_or_imprecise_dtypes=True).then_inc(s_cst, 1)
            pool.iota(iota_bc[:, :, :], [[1, NB], [0, C]], base=0, channel_multiplier=0,
                      allow_small_or_imprecise_dtypes=True).then_inc(s_cst, 1)
            pool.iota(iota_l[:, :], [[1, L]], base=0, channel_multiplier=0,
                      allow_small_or_imprecise_dtypes=True).then_inc(s_cst, 1)
            pool.iota(tile_iota[:, :], [[1, NT]], base=0, channel_multiplier=0,
                      allow_small_or_imprecise_dtypes=True).then_inc(s_cst, 1)
            pool.iota(iota_p[:, :], [[R, P]], base=0, channel_multiplier=0,
                      allow_small_or_imprecise_dtypes=True).then_inc(s_cst, 1)
            pool.iota(iota_c[:, :, :], [[1, LC], [0, C]], base=0, channel_multiplier=0,
                      allow_small_or_imprecise_dtypes=True).then_inc(s_cst, 1)
            pool.iota(block_at[:, :], [[R, NK * P]], base=0, channel_multiplier=0,
                      allow_small_or_imprecise_dtypes=True).then_inc(s_cst, 1)
            pool.iota(block_id[:, :], [[P, NK]], base=0, channel_multiplier=1,
                      allow_small_or_imprecise_dtypes=True).then_inc(s_cst, 1)
            pool.wait_ge(s_cst, 12)
            pool.affine_select(out=ident[:, :], in_=ident[:, :], compare_op=ALU.not_equal, fill=1.0, base=0,
                               pattern=[[-1, P]], channel_multiplier=1).then_inc(s_cst, 1)
            pool.affine_select(out=lower[:, :], in_=onesb[:, :], compare_op=ALU.is_gt, fill=0.0, base=0,
                               pattern=[[1, P]], channel_multiplier=-1).then_inc(s_cst, 1)

            def opened(n, waits):
                pool.wait_ge(s_gate, n + 1)
                for s, v in waits:
                    ge(pool, s, v)
                pool.tensor_tensor(gate[:, 0:1], gate[:, 1:2], gate[:, 1:2], ALU.add).then_inc(s_gate, 1)

            pool.sem_inc(s_free, 2)
            pool.wait_ge(s_zero, 16)
            with pool.Fori(0, GR) as g:
                opened(g, [(s_gev, g + 2), (s_to, g + 1)])
                for k in range(NK):
                    pool.indirect_dma_start(slots, bass.IndirectOffsetOnAxis(block_to[:, k:k + 1], 0),
                                            moved[:, k * R:(k + 1) * R, :].rearrange("p r w -> p (r w)"), None,
                                            bounds_check=NT * P // R - 1, oob_is_err=False).then_inc(s_sct, 16)
                pool.wait_ge(s_free, g + 2)
                pool.wait_ge(s_sct, 16 * NK * (g + 1))
                pool.tensor_tensor(gate[:, 2:3], gate[:, 1:2], gate[:, 1:2], ALU.add).then_inc(s_free, 1)

            def gather_step(layer, source, c, h):
                opened(GR + NST * layer + c, [(s_mr, NST * layer + c + 1)] +
                       ([(s_mm, NT * layer + T * (c - 1))] if not (isinstance(c, int) and c < 2) else []))
                for u in range(T):
                    s = h * T + u
                    pool.indirect_dma_start(msg[:, s, :], None, source,
                                            bass.IndirectOffsetOnAxis(cring[:, s:s + 1], 0)).then_inc(s_g[s], 16)

            for layer, source in enumerate((emb, table1)):
                if layer:
                    pool.wait_ge(s_t1w, 16 * (NB // GRP))
                for c in range(2):
                    gather_step(layer, source, c, c)
                with pool.Fori(1, NST // 2) as i:
                    for h in range(2):
                        gather_step(layer, source, 2 * i + h, h)

            pool.wait_ge(s_cw, 16 * (NB // GRP))
            pool.wait_ge(s_sid, 1)
            for bt in range(BT):
                half = bt % 2
                if bt >= 2:
                    pool.wait_ge(s_ss, bt - 1)
                for l in range(L):
                    pool.indirect_dma_start(seq[:, half, l, :], None, combined,
                                            bass.IndirectOffsetOnAxis(sidi[:, l, bt:bt + 1], 0)
                                            ).then_inc(s_sq[half * NG + l // LG], 16)

        @block.scalar
        def _(act):
            for dst, src in ((it_i, items), (al_i, alias), (in_i, inputs)):
                act.dma_start(dst[:, :, :], src.rearrange("(b p) l -> p b l", p=P)).then_inc(s_sess, 16)
            act.dma_start(w1a[:, :], w_1[0:D, :]).then_inc(s_wts, 16)
            act.dma_start(w1b[:, :], w_1[D:2 * D, :]).then_inc(s_wts, 16)
            act.dma_start(w2c[:, :], w_2).then_inc(s_wts, 16)
            act.dma_start(g1[:, :], glu1_w).then_inc(s_wts, 16)
            act.dma_start(g2[:, :], glu2_w).then_inc(s_wts, 16)
            act.dma_start(b1c[:, :], glu1_b.rearrange("(p o) -> p o", o=1)).then_inc(s_wts, 16)
            act.dma_start(erow[:, :], emb[0:L, :]).then_inc(s_wts, 16)
            act.wait_ge(s_wT, 3)
            act.copy(g1T[:, :], bank[5][:, 0:D]).then_inc(s_wTc, 1)
            act.copy(g2T[:, :], bank[5][:, D:2 * D]).then_inc(s_wTc, 1)
            act.copy(eT[:, :], bank[5][:, 2 * D:2 * D + L]).then_inc(s_wTc, 1)
            act.wait_ge(s_pos, 1)
            act.copy(posb[:, :], bank[6][:, 0:L]).then_inc(s_posc, 1)
            def evacuate():
                act.copy(moved[:, :, :].rearrange("p c w -> p w c"),
                         bank[4][:, 0:2 * LC].rearrange("p (w c) -> p w c", w=2)).then_inc(s_gev, 1)

            act.wait_ge(s_init, 5)
            with act.Fori(0, GR) as g:
                for s in range(SG):
                    n, h = SG * g + s, s % 2
                    act.wait_ge(s_hc, n + 2)
                    act.wait_ge(s_pm, n + 2)
                    act.copy(idle[:, h:h + 1], ones[:, 0:1])
                    for t in range(C):
                        if s == 0 and t == C // 2:
                            act.wait_ge(s_pm, SG * g + 3)
                            act.wait_ge(s_free, g + 1)
                            evacuate()
                        for q, what in enumerate((code, e_val)):
                            last = act.activation(at_c[:, h, t, q, :], hot_c[:, h, :, t], ACT.Copy,
                                                  scale=what[:, bass.ds(n * C + t, 1)])
                        last.then_inc(s_val, 1)
            act.wait_ge(s_pm, SG * GR + 3)
            act.wait_ge(s_free, GR + 1)
            evacuate()
            for m in range(-(-NT // P)):
                w = min(P, NT - P * m)
                act.wait_ge(s_mtr, m + 1)
                act.copy(m_val[:, m * P:m * P + w], bank[2 + m % 2][:, 0:w]).then_inc(s_mta, 1)
            for g in range(0, NB, 2):
                act.wait_ge(s_t1, g + 1)
                act.copy(big[:, 2 * D * g:2 * D * (g + 1)], bank[5][:, 0:2 * D]).then_inc(s_t1a, 1)
            for g in range(NB):
                act.wait_ge(s_g2r, g + 1)
                for q in range(2):
                    ge(act, s_ssq, 2 * g + q - 1)
                    act.activation(sqj[:, q, :], acc[:, (2 * g + q) * D:(2 * g + q + 1) * D], ACT.Square,
                                   scale=1.0 / (LAYERS + 1), accum_out=ssq[:, 2 * g + q:2 * g + q + 1]).then_inc(s_ssq, 1)
            act.wait_ge(s_ssq, 2 * NB)
            act.activation(ginv[:, :], ssq[:, :], ACT.Sqrt).then_inc(s_nrm, 1)
            act.wait_ge(s_gi, 3)
            for g in range(NB):
                ge(act, s_gnT, g - 1)
                for q in range(2):
                    last = act.activation(gnr[:, g % 2, q, :], acc[:, (2 * g + q) * D:(2 * g + q + 1) * D], ACT.Copy,
                                          scale=ginv2[:, 2 * g + q:2 * g + q + 1])
                last.then_inc(s_gn, 1)

            def tanh_step(bt, k):
                m, w = NG * bt + k, min(LG, L - LG * k)
                act.wait_ge(s_z, m + 1)
                ge(act, s_y, NG * (bt - 1) + k + 1)
                for j in range(w):
                    l = LG * k + j
                    last = act.activation(nh1[:, l * P:(l + 1) * P], bank[2 + m % 2][:, j * P:(j + 1) * P],
                                          ACT.Tanh, bias=posb[:, L - 1 - l:L - l])
                last.then_inc(s_th, 1)

            def read_in(bt, k):
                if bt == BT:
                    return
                m, w = NG * bt + k, min(LG, L - LG * k)
                if k < NG:
                    act.wait_ge(s_x, m + 1)
                    ge(act, s_z, m - 1)
                    act.copy(xT[:, m % 2, 0:w * P], bank[m % 2][:, 0:w * P]).then_inc(s_xc, 1)
                if k:
                    tanh_step(bt, k - 1)

            for k in range(NG + 1):
                read_in(0, k)
            for bt in range(BT):
                act.wait_ge(s_hT, bt + 1)
                act.copy(hsT[:, :], bank[4][:, P:2 * P]).then_inc(s_hsc, 1)
                for k in range(NG):
                    m, w = NG * bt + k, min(LG, L - LG * k)
                    act.wait_ge(s_ya, m + 1)
                    ge(act, s_bt, m - 1)
                    act.activation(nh2[:, m % 2, 0:w * P], ysum[:, m % 2, 0:w * P], ACT.Sigmoid).then_inc(s_sg, 1)
                    if k % 4 == 3:
                        read_in(bt + 1, k // 4)
                act.wait_ge(s_sn, 5 * bt + 1)
                act.activation(rown[:, 1:2], rown[:, 0:1], ACT.Sqrt).then_inc(s_sn, 1)
                for n in range(NS):
                    if n % 2:
                        if NG // 4 + n // 2 <= NG:
                            read_in(bt + 1, NG // 4 + n // 2)
                        continue
                    m = (-(-NS // 2)) * bt + n // 2
                    w = 512 if n < NS - 1 else REM
                    act.wait_ge(s_sc, NS * bt + n + 1)
                    ge(act, s_out[m % 4], 16 * (m // 4))
                    act.copy(ostage[:, m % 4, 0:w], bank[5][:, 0:w]).then_inc(s_sca, 1)

        @block.vector
        def _(dve):
            dve.memset(e_row[:, COLS:ECOLS], -1).then_inc(s_init, 1)
            dve.memset(e_col[:, COLS:ECOLS], 0).then_inc(s_init, 1)
            dve.memset(e_val[:, COLS:ECOLS], 0.0).then_inc(s_init, 1)
            dve.memset(lstart[:, GR, :], 0.0).then_inc(s_init, 1)
            dve.memset(place_p[:, 1, :], 0.0)
            dve.memset(at_c[:, 1, :, :, :], 0.0)
            dve.memset(place_c[:, 1, :], 0.0).then_inc(s_init, 1)
            chain = [0]

            def link(ins):
                chain[0] += 1
                ins.then_inc(s_v, 1)
                dve.wait_ge(s_v, chain[0])

            dve.wait_ge(s_edge, 96)
            dve.wait_ge(s_init, 5)
            link(dve.tensor_single_scalar(bkt_i, e_row, BUCKET.bit_length() - 1, ALU.arith_shift_right))
            link(dve.tensor_copy(bkt, bkt_i))
            dve.sem_inc(s_red, 1)
            dve.wait_ge(s_cst, 14)
            with dve.Fori(0, GR) as g:
                for s in range(SG):
                    dve.wait_ge(s_h, SG * g + s + 1)
                    dve.tensor_tensor(oh[:, s % 2, :, :], iota_bc[:, :, :],
                                      bkt[:, bass.ds((SG * g + s) * C, C)].unsqueeze(1).broadcast_to([P, NB, C]),
                                      ALU.is_equal).then_inc(s_oh1, 1)
                dve.wait_ge(s_h, SG * (g + 1) + 2)
                dve.wait_ge(s_red, g + 1)
                dve.tensor_reduce(gcnt_now[:, :], octv(4), AX_X, ALU.add).then_inc(s_red, 1)
                dve.wait_ge(s_red, g + 2)
                dve.tensor_copy(gcnt[:, bass.ds(g, 1), :], gcnt_now[:, :].unsqueeze(1)).then_inc(s_v, 1)
            chain[0] += GR
            dve.wait_ge(s_v, chain[0])
            link(dve.tensor_scalar(gpad_i[:, :, :], gcnt[:, :, :], float(R - 1), None, ALU.add))
            link(dve.tensor_single_scalar(gpad_j[:, :, :], gpad_i[:, :, :], -R, ALU.bitwise_and))
            link(dve.tensor_copy(gpad[:, :, :], gpad_j[:, :, :]))
            for g in range(GR):
                last = dve.tensor_tensor_scan(gcum[:, g, :], ones[:, 0:NB], gpad[:, g, :], 0.0, ALU.mult, ALU.add)
            link(last)
            dve.tensor_copy(lstart[:, 0:GR, NB:NB + 1], gcum[:, :, NB - 1:NB])
            link(dve.tensor_tensor(lstart[:, 0:GR, 0:NB], gcum[:, :, :], gpad[:, :, :], ALU.subtract))
            link(dve.tensor_reduce(tot[:, :], gpad[:, :, :].rearrange("p g b -> p b g"), AX_X, ALU.add))
            link(dve.tensor_scalar(toti[:, :], tot[:, :], float(P - 1), None, ALU.add))
            link(dve.tensor_single_scalar(toti2[:, :], toti[:, :], P.bit_length() - 1, ALU.arith_shift_right))
            link(dve.tensor_copy(ntile[:, :], toti2[:, :]))
            link(dve.tensor_tensor_scan(cum[:, :], ones[:, 0:NB], ntile[:, :], 0.0, ALU.mult, ALU.add))
            link(dve.tensor_tensor(start[:, :], cum[:, :], ntile[:, :], ALU.subtract))
            link(dve.tensor_scalar(gofs[:, 0, :], start[:, :], float(P), None, ALU.mult))
            for g in range(1, GR):
                link(dve.tensor_tensor(gofs[:, g, :], gofs[:, g - 1, :], gpad[:, g - 1, :], ALU.add))
            dve.memset(delta[:, :, NB:NB + 1], FAR)
            link(dve.tensor_tensor(delta[:, :, 0:NB], gofs[:, :, :], lstart[:, 0:GR, 0:NB], ALU.subtract))
            link(dve.tensor_scalar(delta[:, :, :], delta[:, :, :], 1.0 / R, None, ALU.mult))
            dve.tensor_copy(dstep[:, :, 0:1], delta[:, :, 0:1])
            dve.tensor_tensor(dstep[:, :, 1:NB + 1], delta[:, :, 1:NB + 1], delta[:, :, 0:NB], ALU.subtract).then_inc(s_ls, 1)
            link(dve.tensor_tensor_reduce(junkb[0:NB, :], start[0:NB, :], ident[0:NB, 0:NB], 1.0, 0.0,
                                          ALU.mult, ALU.add, startc[0:NB, :]))
            dve.tensor_scalar(tile_ge[0:NB, :], tile_iota[0:NB, :], startc[0:NB, 0:1], None, ALU.is_ge).then_inc(s_tge, 1)
            dve.wait_ge(s_lc, 1)
            dve.tensor_copy(lscol[:, :], bank[5][0:NB + 1, 0:GR])
            dve.tensor_copy(dscol[:, :], bank[5][0:NB + 1, GR:2 * GR]).then_inc(s_lcc, 1)
            dve.wait_ge(s_tge, 2)
            for n in range(3):
                a, b = n * TW, min(NT, (n + 1) * TW)
                dve.tensor_scalar(tile_off[0:1, a:b], bank[5 + n][0:1, 0:b - a], -1.0, float(BUCKET),
                                  ALU.add, ALU.mult).then_inc(s_toff, 1)
            link(dve.tensor_single_scalar(bkt_i, e_row, BUCKET - 1, ALU.bitwise_and))
            link(dve.tensor_scalar(col_f, e_col, 0.0, float(N - 1), ALU.max, ALU.min))
            link(dve.scalar_tensor_tensor(code, col_f, float(BUCKET), bkt_i, ALU.mult, ALU.add))
            link(dve.scalar_tensor_tensor(code, bkt, 0.0, code, ALU.is_ge, ALU.mult))
            dve.wait_ge(s_sess, 48)
            dve.tensor_copy(al_f[:, :, :], al_i[:, :, :])
            link(dve.tensor_copy(it_f[:, :, :], it_i[:, :, :]))
            link(dve.tensor_scalar(it_n[:, :, :], it_f[:, :, :], 0.0, float(N), ALU.is_lt, ALU.mult))
            link(dve.tensor_tensor(it_f[:, :, :], it_f[:, :, :], it_n[:, :, :], ALU.add))
            link(dve.tensor_scalar(it_n[:, :, :], it_f[:, :, :], 0.0, float(N - 1), ALU.max, ALU.min))
            link(dve.tensor_scalar(mask[:, :, :], in_i[:, :, :], 0.0, None, ALU.not_equal))
            link(dve.tensor_reduce(mcnt[:, :], mask[:, :, :], AX_X, ALU.add))
            link(dve.reciprocal(mrec[:, :], mcnt[:, :]))
            for bt in range(BT):
                link(dve.tensor_scalar(maskn[:, bt, :], mask[:, bt, :], mrec[:, bt:bt + 1], None, ALU.mult))

            def build(n, h):
                dve.tensor_tensor(oh[:, h, :, :], iota_bc[:, :, :],
                                  bkt[:, bass.ds(n * C, C)].unsqueeze(1).broadcast_to([P, NB, C]),
                                  ALU.is_equal).then_inc(s_oh, 1)

            def hot_columns(n, h):
                dve.wait_ge(s_val, C * n + 1)
                dve.tensor_tensor(hot_c[:, h, :, :], iota_c[:, :, :],
                                  place_c[:, h, :].unsqueeze(1).broadcast_to([P, LC, C]), ALU.is_equal).then_inc(s_hc, 1)

            def hot_partitions(n, h, part):
                t = slice(part * C // 2, (part + 1) * C // 2)
                if part == 0:
                    dve.wait_ge(s_pm, n + 1)
                dve.tensor_tensor(at_p[:, h, t, :], iota_p[:, :].unsqueeze(1).broadcast_to([P, C // 2, P]),
                                  place_p[:, h, t].unsqueeze(2).broadcast_to([P, C // 2, P]),
                                  ALU.is_equal).then_inc(s_hp, 1)

            def sort_step(g, s, v):
                n, h = SG * g + s, s % 2
                dve.wait_ge(s_rank, n + 1)
                if s < SG - 1:
                    dve.tensor_tensor(base[:, 1 - h, :], base[:, h, :], bank[2 + h][:, 0:NB], ALU.add).then_inc(s_base, 1)
                else:
                    dve.tensor_copy(base[:, 1 - h, :], lstart[:, bass.ds(g + 1, 1), 0:NB].rearrange("p o b -> p (o b)")
                                    ).then_inc(s_base, 1)
                dve.tensor_tensor(rank[:, :, :], octv(h), oh[:, h, :, :], ALU.mult).then_inc(s_rel, 1)
                dve.wait_ge(s_v, v)
                hot_columns(n, 1 - h)
                dve.wait_ge(s_rel, n + 3)
                dve.tensor_reduce(posf[:, :], rank[:, :, :].rearrange("p b t -> p t b"), AX_X, ALU.add).then_inc(s_v, 1)
                hot_partitions(n, 1 - h, 0)
                dve.wait_ge(s_v, v + 1)
                dve.tensor_copy(posi[:, :], posf[:, :]).then_inc(s_v, 1)
                hot_partitions(n, 1 - h, 1)
                dve.wait_ge(s_v, v + 2)
                dve.tensor_single_scalar(place_i[:, 0, :], posi[:, :], (P - 1) * R, ALU.bitwise_and)
                dve.tensor_scalar(place_i[:, 1, :], posi[:, :], P.bit_length() - 1, -R,
                                  ALU.arith_shift_right, ALU.bitwise_and)
                dve.tensor_single_scalar(place_i[:, 2, :], posi[:, :], R - 1, ALU.bitwise_and).then_inc(s_v, 1)
                build(n + 2, h)
                dve.wait_ge(s_v, v + 3)
                dve.tensor_copy(place_p[:, h, :], place_i[:, 0, :])
                dve.tensor_tensor(place_c[:, h, :], place_i[:, 1, :], place_i[:, 2, :], ALU.add).then_inc(s_v, 1)

            def targets(g, part):
                if part == 0:
                    dve.tensor_copy(dsnow[:, :], dscol[:, bass.ds(g, 1)])
                    dve.tensor_scalar(begun[0:NB + 1, :], block_at[0:NB + 1, :], lscol[:, bass.ds(g, 1)], None,
                                      ALU.is_ge).then_inc(s_bg, 1)
                else:
                    dve.wait_ge(s_dst, g + 1)
                    dve.wait_ge(s_free, g + 2)
                    dve.tensor_tensor(block_to[:, :], bank[7][:, 0:NK], block_id[:, :], ALU.add).then_inc(s_to, 1)

            def session_rows(l):
                for bt in range(BT):
                    dve.scalar_tensor_tensor(junkl[:, bt, :], iota_l[:, :], al_f[:, bt, bass.ds(l, 1)], it_n[:, bt, :],
                                             ALU.is_equal, ALU.mult, accum_out=sidf[:, bass.ds(l, 1), bt])

            v0 = chain[0]
            dve.wait_ge(s_lcc, 1)
            dve.sem_inc(s_rel, 2)
            dve.tensor_copy(base[:, 0, :], lstart[:, 0, 0:NB]).then_inc(s_base, 1)
            build(0, 0)
            build(1, 1)
            dve.sem_inc(s_val, 2 * C + 1)
            with dve.Fori(0, GR) as g:
                for s in range(SG):
                    sort_step(g, s, v0 + 4 * (SG * g + s))
                    if s == 1:
                        targets(g, 0)
                    if s == 8:
                        targets(g, 1)
            chain[0] = v0 + 4 * SG * GR
            dve.wait_ge(s_v, chain[0])
            hot_columns(SG * GR, 1)
            hot_partitions(SG * GR, 1, 0)
            hot_partitions(SG * GR, 1, 1)
            with dve.Fori(0, L) as i:
                dve.wait_ge(s_v, v0 + 4 * SG * GR + i)
                session_rows(i)
                dve.tensor_copy(prime[:, :], iota_l[:, 0:1]).then_inc(s_v, 1)
            chain[0] += L
            dve.wait_ge(s_v, chain[0])
            dve.tensor_copy(sidi[:, :, :], sidf[:, :, :]).then_inc(s_sid, 1)

            for m in range(-(-NT // P)):
                w = min(P, NT - P * m)
                dve.wait_ge(s_mtr, m + 1)
                dve.tensor_copy(m_code[:, m * P:m * P + w], bank[m % 2][:, 0:w]).then_inc(s_mtc, 1)
            dve.wait_ge(s_mtc, -(-NT // P))
            dve.tensor_single_scalar(m_col, m_code, BUCKET.bit_length() - 1, ALU.arith_shift_right)
            link(dve.tensor_single_scalar(m_code, m_code, BUCKET - 1, ALU.bitwise_and))
            link(dve.tensor_copy(m_lo, m_code))
            dve.wait_ge(s_mta, -(-NT // P))

            def fetch(c, h, layer):
                dve.tensor_copy(mlo[:, h * T:(h + 1) * T], m_lo[:, bass.ds(c * T, T)])
                dve.tensor_copy(mval[:, h * T:(h + 1) * T], m_val[:, bass.ds(c * T, T)])
                dve.tensor_copy(cring[:, h * T:(h + 1) * T], m_col[:, bass.ds(c * T, T)]).then_inc(s_mr, 1)

            def one_hot(u):
                dve.tensor_scalar(onehot[:, u % SR, :], iota_r[:, :], mlo[:, u:u + 1], mval[:, u:u + 1],
                                  ALU.is_equal, ALU.mult).then_inc(s_S, 1)

            def round_step(layer, c, h, last=False):
                if not last:
                    fetch(c + 1, 1 - h, layer)
                for u in range(T):
                    j = NT * layer + T * c + u
                    dve.wait_ge(s_mm, j + 1)
                    if not last or u + SR < T:
                        if u + SR == T:
                            dve.wait_ge(s_mr, NST * layer + c + 2)
                        one_hot((h * T + u + SR) % (2 * T))
                    off = dve.value_load(tile_off[0:1, bass.ds(T * c + u, 1)], min_val=0, max_val=ROWS - BUCKET)
                    dve.wait_ge(s_acc, j + 1)
                    dve.tensor_tensor(acc[:, bass.ds(off, BUCKET)], acc[:, bass.ds(off, BUCKET)],
                                      bank[u % PR][:, 0:BUCKET], ALU.add).then_inc(s_acc, 1)

            dve.sem_inc(s_acc, 1)
            dve.wait_ge(s_zero, 16)
            for layer in range(LAYERS):
                if layer:
                    dve.wait_ge(s_mm, NT)
                fetch(0, 0, layer)
                dve.wait_ge(s_mr, NST * layer + 1)
                for u in range(SR):
                    one_hot(u)
                with dve.Fori(0, NST // 2 - 1) as i:
                    for h in range(2):
                        round_step(layer, 2 * i + h, h)
                round_step(layer, NST - 2, 0)
                round_step(layer, NST - 1, 1, last=True)
                if layer == 0:
                    for g in range(1, NB, 2):
                        dve.wait_ge(s_t1, g + 1)
                        dve.tensor_copy(big[:, 2 * D * g:2 * D * (g + 1)], bank[6][:, 0:2 * D]).then_inc(s_t1v, 1)
                    dve.wait_ge(s_t1w, 16 * (NB // GRP))
                    dve.memset(big_rows[:, emb_full, :], 0.0).then_inc(s_fz, 1)
            dve.memset(feat_rows[:, emb_full, :], 0.0).then_inc(s_fz, 1)

            dve.wait_ge(s_eld, 32)
            for g in range(NB):
                cols = slice(2 * D * g, 2 * D * (g + 1))
                dve.wait_ge(s_t2, g + 1)
                dve.tensor_tensor(acc[:, cols], bank[5 + g % 2][:, 0:2 * D], big[:, cols], ALU.add).then_inc(s_g2r, 1)
                dve.wait_ge(s_g2r, g + 1)
                if g == 0:
                    dve.wait_ge(s_fld, 32)
                dve.scalar_tensor_tensor(big[:, cols], acc[:, cols], 1.0 / (LAYERS + 1), ring[:, cols],
                                         ALU.mult, ALU.add).then_inc(s_cmb, 1)
            dve.wait_ge(s_nrm, 1)
            dve.tensor_scalar(ginv[:, :], ginv[:, :], EPS, None, ALU.max).then_inc(s_gi, 1)
            dve.wait_ge(s_gi, 1)
            dve.reciprocal(ginv[:, :], ginv[:, :]).then_inc(s_gi, 1)
            dve.wait_ge(s_gi, 2)
            dve.tensor_scalar(ginv2[:, :], ginv[:, :], 1.0 / (LAYERS + 1), None, ALU.mult).then_inc(s_gi, 1)
            for g in range(NB):
                dve.wait_ge(s_gnT, g + 1)
                dve.tensor_copy(acc[:, 2 * D * g:2 * D * (g + 1)], bank[5 + g % 2][:, 0:2 * D]).then_inc(s_gnc, 1)
            dve.wait_ge(s_cw, 16 * (NB // GRP))

            def read_in(bt, k):
                if bt == BT or k == NG:
                    return
                dve.wait_ge(s_sq[bt % 2 * NG + k], 16 * min(LG, L - LG * k) * (bt // 2 + 1))
                dve.wait_ge(s_v, chain[0])
                for l in range(LG * k, min(L, LG * k + LG)):
                    if l >= 2:
                        dve.wait_ge(s_v, h_at[l - 2])
                        last = dve.scalar_tensor_tensor(hsum[:, l % 4, :], seq[:, bt % 2, l, :],
                                                        maskn[:, bt, l:l + 1], hsum[:, (l - 2) % 4, :],
                                                        ALU.mult, ALU.add)
                    else:
                        last = dve.tensor_scalar(hsum[:, l, :], seq[:, bt % 2, l, :], maskn[:, bt, l:l + 1],
                                                 None, ALU.mult)
                    last.then_inc(s_v, 1)
                    chain[0] += 1
                    h_at[l] = chain[0]
                if k == NG - 1:
                    dve.wait_ge(s_v, chain[0])
                    if bt:
                        dve.wait_ge(s_hT, bt)
                    dve.tensor_tensor(hrow[:, :], hsum[:, (L - 1) % 4, :], hsum[:, (L - 2) % 4, :],
                                      ALU.add).then_inc(s_hs, 1)

            def weigh(bt, k):
                m, w = NG * bt + k, min(LG, L - LG * k)
                dve.wait_ge(s_bt, m + 1)
                dve.tensor_tensor(beta[:, LG * k:LG * k + w], bank[(4, 7)[m % 2]][:, 0:w],
                                  mask[:, bt, LG * k:LG * k + w], ALU.mult).then_inc(s_bm, 1)
                dve.wait_ge(s_bm, m + 1)
                for l in range(LG * k, LG * k + w):
                    if l >= 2:
                        dve.wait_ge(s_v, e_at[l - 2])
                        last = dve.scalar_tensor_tensor(sess[:, l % 4, :], seq[:, bt % 2, l, :], beta[:, l:l + 1],
                                                        sess[:, (l - 2) % 4, :], ALU.mult, ALU.add)
                    else:
                        last = dve.tensor_scalar(sess[:, l, :], seq[:, bt % 2, l, :], beta[:, l:l + 1], None, ALU.mult)
                    last.then_inc(s_v, 1)
                    chain[0] += 1
                    e_at[l] = chain[0]

            h_at, e_at = {}, {}
            for k in range(NG):
                read_in(0, k)
            for bt in range(BT):
                dve.wait_ge(s_p2, bt + 1)
                dve.tensor_scalar(bias2[:, :], bank[7][:, P:2 * P], b1c[:, 0:1], None, ALU.add).then_inc(s_b2, 1)
                dve.wait_ge(s_b2, bt + 1)
                for k in range(NG):
                    m, w = NG * bt + k, min(LG, L - LG * k)
                    dve.wait_ge(s_y, m + 1)
                    ge(dve, s_sg, m - 1)
                    dve.tensor_tensor(ysum[:, m % 2, 0:w * P].rearrange("p (l n) -> p l n", n=P),
                                      bank[5 + m % 2][:, 0:w * P].rearrange("p (l n) -> p l n", n=P),
                                      bias2[:, :].unsqueeze(1).broadcast_to([P, w, P]), ALU.add).then_inc(s_ya, 1)
                    if k:
                        weigh(bt, k - 1)
                    if k % 4 == 3:
                        read_in(bt + 1, k // 4)
                weigh(bt, NG - 1)
                dve.wait_ge(s_v, chain[0])
                dve.tensor_tensor(junk[:, :], sess[:, (L - 1) % 4, :], sess[:, (L - 2) % 4, :], ALU.add).then_inc(s_ss, 1)
                dve.wait_ge(s_ss, bt + 1)
                dve.tensor_tensor_reduce(sess[:, 0, :], junk[:, :], junk[:, :], 1.0, 0.0, ALU.mult, ALU.add,
                                         rown[:, 0:1]).then_inc(s_sn, 1)
                dve.wait_ge(s_sn, 5 * bt + 2)
                dve.tensor_scalar(rown[:, 2:3], rown[:, 1:2], EPS, None, ALU.max).then_inc(s_sn, 1)
                dve.wait_ge(s_sn, 5 * bt + 3)
                dve.reciprocal(rown[:, 3:4], rown[:, 2:3]).then_inc(s_sn, 1)
                dve.wait_ge(s_sn, 5 * bt + 4)
                dve.tensor_scalar(sess[:, 1, :], junk[:, :], rown[:, 3:4], W_K, ALU.mult, ALU.mult).then_inc(s_sn, 1)
                dve.wait_ge(s_sT, bt + 1)
                dve.tensor_copy(selT[:, :], bank[4][:, 2 * P:3 * P]).then_inc(s_sTc, 1)
                for n in range(1, NS, 2):
                    m = (-(-NS // 2)) * bt + n // 2
                    dve.wait_ge(s_sc, NS * bt + n + 1)
                    ge(dve, s_out[m % 4], 16 * (m // 4))
                    dve.tensor_copy(ostage[:, m % 4, 512:1024], bank[6][:, :]).then_inc(s_scv, 1)
                    if NG // 4 + n // 2 <= NG:
                        read_in(bt + 1, NG // 4 + n // 2)

        @block.tensor
        def _(pe):
            pe.wait_ge(s_wts, 112)
            pe.wait_ge(s_cst, 14)
            pe.transpose(bank[5][:, 0:D], g1[:, :], ident[:, :]).then_inc(s_wT, 1)
            pe.transpose(bank[5][:, D:2 * D], g2[:, :], ident[:, :]).then_inc(s_wT, 1)
            pe.transpose(bank[5][:, 2 * D:2 * D + L], erow[:, :], ident[0:L, 0:L]).then_inc(s_wT, 1)
            pe.wait_ge(s_wTc, 3)
            pe.matmul(bank[6][:, 0:L], w1a[:, :], eT[:, :], start=True, stop=True).then_inc(s_pos, 1)
            pe.wait_ge(s_posc, 1)
            pe.sem_inc(s_h, 2)
            with pe.Fori(0, GR) as g:
                pe.wait_ge(s_red, g + 1)
                for s in range(SG):
                    pe.wait_ge(s_oh1, SG * g + s + 1)
                    pe.matmul(octv(4), onesb[:, :], oh[:, s % 2, :, :], start=(s == 0), stop=(s == SG - 1)).then_inc(s_h, 1)
            pe.wait_ge(s_ls, 1)
            for g in range(GR):
                pe.matmul(bank[5][0:NB + 1, g:g + 1], lstart[0:1, g, :], ones[0:1, 0:1], start=True, stop=True)
                last = pe.matmul(bank[5][0:NB + 1, GR + g:GR + g + 1], dstep[0:1, g, :], ones[0:1, 0:1],
                                 start=True, stop=True)
            last.then_inc(s_lc, 1)
            pe.wait_ge(s_lcc, 1)
            pe.wait_ge(s_tge, 1)
            for n in range(3):
                a, b = n * TW, min(NT, (n + 1) * TW)
                last = pe.matmul(bank[5 + n][0:1, 0:b - a], onesb[0:NB, 0:1], tile_ge[0:NB, a:b], start=True, stop=True)
            last.then_inc(s_tge, 1)
            pe.wait_ge(s_toff, 3)

            def rank_step(n, h):
                pe.wait_ge(s_oh, n + 1)
                pe.wait_ge(s_base, n + 1)
                pe.wait_ge(s_rel, n + 1)
                pe.matmul(octv(h), ones[0:1, 0:P], base[0:1, h, :].unsqueeze(2).broadcast_to([1, NB, C]),
                          start=True, stop=False, skip_group_check=True)
                pe.matmul(octv(h), lower[:, :], oh[:, h, :, :], start=False, stop=False, skip_group_check=True)
                for k in range(1, C):
                    pe.matmul(octv(h)[:, :, k:C], onesb[:, :], oh[:, h, :, 0:C - k], start=False, stop=(k == C - 1),
                              skip_group_check=True)
                for t in range(C):
                    last = pe.matmul(bank[2 + h][:, 0:NB], onesb[:, :], oh[:, h, :, t], start=(t == 0), stop=(t == C - 1))
                last.then_inc(s_rank, 1)

            def permute(n, h, s):
                for t in range(C):
                    if t % (C // 2) == 0:
                        pe.wait_ge(s_hp, 2 * n + t // (C // 2) + 1)
                    pe.wait_ge(s_val, C * (n + 1) + t + 2)
                    last = pe.matmul(bank[4][:, 0:2 * LC], at_p[:, h, t, :],
                                     at_c[:, h, t, :, :].rearrange("p w c -> p (w c)"),
                                     start=(s == 1 and t == 0), stop=(s == 0 and t == C - 1),
                                     skip_group_check=True)
                last.then_inc(s_pm, 1)

            pe.sem_inc(s_pm, 2)
            rank_step(0, 0)
            with pe.Fori(0, GR) as g:
                for s in range(SG):
                    n, h = SG * g + s, s % 2
                    rank_step(n + 1, 1 - h)
                    if s == 1:
                        pe.wait_ge(s_gev, g + 1)
                    permute(n, 1 - h, s)
                    if s == 3:
                        pe.wait_ge(s_bg, g + 1)
                        for k in range(NK):
                            last = pe.matmul(bank[7][:, k:k + 1], begun[0:NB + 1, k * P:(k + 1) * P], dsnow[:, :],
                                             start=True, stop=True)
                        last.then_inc(s_dst, 1)
            permute(SG * GR, 1, 0)
            pe.wait_ge(s_meta, 32)
            pe.wait_ge(s_rel, 2 + SG * GR)
            for m in range(-(-NT // P)):
                w = min(P, NT - P * m)
                ge(pe, s_mtc, m - 1)
                ge(pe, s_mta, m - 1)
                for q in range(2):
                    last = pe.transpose(bank[2 * q + m % 2][:, 0:w], sorted_rows[0:w, m, :, q], ident[0:w, 0:w])
                last.then_inc(s_mtr, 1)

            def products(layer, c, it, h):
                for u in range(T):
                    j = NT * layer + T * c + u
                    pe.wait_ge(s_g[h * T + u], 16 * ((NST // 2) * layer + it + 1))
                    pe.wait_ge(s_S, j + 1)
                    ge(pe, s_acc, j + 2 - PR)
                    pe.matmul(bank[u % PR][:, 0:BUCKET], msg[:, h * T + u, :], onehot[:, u % SR, :],
                              start=True, stop=True).then_inc(s_mm, 1)

            for layer in range(LAYERS):
                for c in range(2):
                    products(layer, c, 0, c)
                with pe.Fori(1, NST // 2) as i:
                    for h in range(2):
                        products(layer, 2 * i + h, i, h)
                pe.wait_ge(s_acc, NT * (layer + 1) + 1)
                for g in range(NB):
                    if layer == 0:
                        ge(pe, (s_t1a, s_t1v)[g % 2], g // 2)
                    else:
                        ge(pe, s_g2r, g - 1)
                    for q in range(2):
                        last = pe.transpose(bank[5 + g % 2][:, q * D:(q + 1) * D],
                                            acc[:, (2 * g + q) * D:(2 * g + q + 1) * D], ident[:, :])
                    last.then_inc((s_t1, s_t2)[layer], 1)
            for g in range(NB):
                pe.wait_ge(s_gn, g + 1)
                if g < 2:
                    pe.wait_ge(s_g2r, NB)
                ge(pe, s_gnc, g - 1)
                for q in range(2):
                    last = pe.transpose(bank[5 + g % 2][:, q * D:(q + 1) * D], gnr[:, g % 2, q, :], ident[:, :])
                last.then_inc(s_gnT, 1)

            def first_product(bt, k):
                m, w = NG * bt + k, min(LG, L - LG * k)
                pe.wait_ge(s_xc, m + 1)
                ge(pe, s_th, m - 1)
                pe.matmul(bank[2 + m % 2][:, 0:w * P], w1b[:, :], xT[:, m % 2, 0:w * P],
                          start=True, stop=True).then_inc(s_z, 1)

            def read_in(bt, k):
                if bt == BT:
                    return
                m, w = NG * bt + k, min(LG, L - LG * k)
                if k < NG:
                    pe.wait_ge(s_sq[bt % 2 * NG + k], 16 * w * (bt // 2 + 1))
                    ge(pe, s_xc, m - 1)
                    for j in range(w):
                        last = pe.transpose(bank[m % 2][:, j * P:(j + 1) * P], seq[:, bt % 2, LG * k + j, :],
                                            ident[:, :])
                    last.then_inc(s_x, 1)
                if k:
                    first_product(bt, k - 1)

            def read_out(bt, k):
                m, w = NG * bt + k, min(LG, L - LG * k)
                pe.wait_ge(s_sg, m + 1)
                ge(pe, s_bm, m - 1)
                for j in range(w):
                    last = pe.matmul(bank[(4, 7)[m % 2]][:, j:j + 1], nh2[:, m % 2, j * P:(j + 1) * P], w2c[:, :],
                                     start=True, stop=True)
                last.then_inc(s_bt, 1)

            for k in range(NG + 1):
                read_in(0, k)
            for bt in range(BT):
                pe.wait_ge(s_hs, bt + 1)
                if bt:
                    pe.wait_ge(s_sTc, bt)
                pe.transpose(bank[4][:, P:2 * P], hrow[:, :], ident[:, :]).then_inc(s_hT, 1)
                pe.wait_ge(s_hsc, bt + 1)
                pe.matmul(bank[7][:, P:2 * P], g2T[:, :], hsT[:, :], start=True, stop=True).then_inc(s_p2, 1)
                for k in range(NG):
                    m, w = NG * bt + k, min(LG, L - LG * k)
                    pe.wait_ge(s_th, m + 1)
                    if k < 2:
                        pe.wait_ge(s_gnc, NB)
                        ge(pe, s_sca, (-(-NS // 2)) * bt)
                        ge(pe, s_scv, (NS // 2) * bt)
                    else:
                        pe.wait_ge(s_ya, m - 1)
                    pe.matmul(bank[5 + m % 2][:, 0:w * P], g1T[:, :], nh1[:, k * LG * P:(k * LG + w) * P],
                              start=True, stop=True).then_inc(s_y, 1)
                    if k:
                        if k == 1:
                            pe.wait_ge(s_b2, bt + 1)
                        read_out(bt, k - 1)
                    if k % 4 == 3:
                        read_in(bt + 1, k // 4)
                read_out(bt, NG - 1)
                pe.wait_ge(s_bm, NG * (bt + 1))
                pe.wait_ge(s_sn, 5 * (bt + 1))
                pe.transpose(bank[4][:, 2 * P:3 * P], sess[:, 1, :], ident[:, :]).then_inc(s_sT, 1)
                pe.wait_ge(s_sTc, bt + 1)
                for n in range(NS):
                    w = 512 if n < NS - 1 else REM
                    if n < 2:
                        pe.wait_ge(s_ya, NG * (bt + 1))
                    elif n % 2:
                        pe.wait_ge(s_scv, (NS // 2) * bt + n // 2)
                    else:
                        pe.wait_ge(s_sca, (-(-NS // 2)) * bt + n // 2)
                    pe.matmul(bank[5 + n % 2][:, 0:w], selT[:, :], acc[:, 512 * n:512 * n + w],
                              start=True, stop=True).then_inc(s_sc, 1)
                    if n % 2 and NG // 4 + n // 2 <= NG:
                        read_in(bt + 1, NG // 4 + n // 2)


_INS = ["r_items", "r_inputs", "r_alias_inputs", "L0_rec_item_features", "L0_rec_adj_row", "L0_rec_adj_col",
        "L0_rec_adj_val", "L0_rec_emb", "L0_rec_w_1", "L0_rec_w_2", "L0_rec_glu1_w", "L0_rec_glu1_b", "L0_rec_glu2_w"]


def kernel(**inputs):
    import numpy as _np
    import concourse.bacc as _bacc
    from concourse import mybir as _mybir
    from concourse.bass_utils import run_bass_kernel_spmd as _run

    nc = _bacc.Bacc("TRN2", target_bir_lowering=False, num_devices=1)
    arrays, args = {}, []
    for name in _INS:
        a = _np.ascontiguousarray(inputs[name])
        arrays[f"in_{name}"] = a
        args.append(nc.dram_tensor(f"in_{name}", a.shape, _mybir.dt.from_np(a.dtype), kind="ExternalInput").ap())
    shape = (inputs["r_items"].shape[0], inputs["L0_rec_emb"].shape[0])
    args.append(nc.dram_tensor("scores", shape, _mybir.dt.float32, kind="ExternalOutput").ap())
    recommender_program(nc, *args)
    r = _run(nc, [arrays], core_ids=[0])
    return r.results[0]["scores"]
```

```python
from contextlib import ExitStack

import concourse.bass as bass
from concourse import mybir

ALU = mybir.AluOpType
ACT = mybir.ActivationFunctionType
AX_X = mybir.AxisListType.X
F32 = mybir.dt.float32
BF16 = mybir.dt.bfloat16
I32 = mybir.dt.int32

P = 128
W_K = 12.0
EPS = 1e-12
LAYERS = 2


def ge(eng, sem, value):
    if isinstance(value, int) and value <= 0:
        return
    eng.wait_ge(sem, value)


def recommender_program(nc, items, inputs, alias, features, adj_row, adj_col, adj_val, emb,
                        w_1, w_2, glu1_w, glu1_b, glu2_w, out):
    B, L = items.shape
    N, D = emb.shape
    E = adj_row.shape[0]
    BT = B // P
    BUCKET = 256
    NB = -(-N // BUCKET)
    ROWS = NB * BUCKET
    COLS = E // P
    TAIL = E - COLS * P
    C = 8
    SG = 8
    GR = -(-(COLS + 1) // (C * SG))
    R = 4
    NK = -(-(SG * C * P + NB * (R - 1)) // (R * P))
    LC = NK * R
    Q = 4
    ECOLS = (GR * SG + Q) * C
    T = 24
    NT = -(-((E + GR * NB * (R - 1) + NB * (P - 1)) // P) // T) * T
    NST = NT // T
    FAR = float(2 ** 20)
    SR, PR = 8, 4
    assert NST % 2 == 0 and SG % Q == 0 and D == P and 0 < TAIL < P and T % SR == 0 and SR % PR == 0
    LOOP = 2 * min(NST // 2 - 1, L // 2, NB // 2)
    LG = 4
    NG = -(-L // LG)
    NR = 4
    NS = -(-N // 512)
    REM = N - (NS - 1) * 512
    assert 2 * NG >= NS
    TW = -(-NT // 3)

    with ExitStack() as ctx:
        def sb(name, shape, dt=F32):
            return ctx.enter_context(nc.sbuf_tensor(name, shape, dt))

        def sem(name):
            return ctx.enter_context(nc.semaphore(name))

        slots = nc.dram_tensor("sorted_edges", [NT * P // R, 2 * R], F32).ap()
        table1 = nc.dram_tensor("table1", [ROWS, D], F32).ap()
        combined = nc.dram_tensor("combined", [ROWS, D], F32).ap()

        acc = sb("acc", [P, ROWS])
        big = sb("big", [P, ROWS])
        ring = sb("ring", [P, 2 * L * D])
        at = [0]

        def carve(base, words, dt=F32):
            v = base[:, at[0]:at[0] + words]
            at[0] += words
            return v if dt == F32 else v.bitcast(dt)

        e_row = carve(big, ECOLS, I32)
        e_col = carve(big, ECOLS, I32)
        bkt_i = carve(big, ECOLS, I32)
        col_f = carve(big, ECOLS)
        e_val = carve(big, ECOLS)
        bkt = carve(big, ECOLS // 2, BF16)
        code = carve(big, ECOLS)
        at_c = big[:, 0:Q * C * 2 * LC].rearrange("p (h t w n) -> p h t w n", h=Q, t=C, w=2)
        assert Q * C * 2 * LC <= 4 * ECOLS
        block_at = carve(big, NK * P)
        iota_c = carve(big, LC * C // 2, BF16).rearrange("p (c t) -> p c t", t=C)
        hot_c = carve(big, Q * LC * C // 2, BF16).rearrange("p (h c t) -> p h c t", h=Q, t=C)
        assert at[0] <= ROWS
        at[0] = 0
        tile_iota = carve(ring, NT)
        tile_ge = carve(ring, NT // 2, BF16)
        oh1 = ring[:, at[0]:at[0] + Q * NB * C // 2].bitcast(BF16).rearrange("p (h b t) -> p h b t", h=Q, t=C)
        at_p = carve(ring, Q * C * P).rearrange("p (h t n) -> p h t n", h=Q, t=C)
        begun = carve(ring, NK * P)
        gofs = carve(ring, GR * NB).rearrange("p (g b) -> p g b", g=GR)
        delta = carve(ring, GR * (NB + 1)).rearrange("p (g b) -> p g b", g=GR)
        dstep = carve(ring, GR * (NB + 1)).rearrange("p (g b) -> p g b", g=GR)
        rank = carve(ring, NB * C).rearrange("p (b t) -> p b t", t=C)
        assert at[0] <= 2 * L * D
        sorted_rows = big[:, 0:-(-NT // P) * 2 * P].rearrange("p (m s w) -> p m s w", w=2, s=P)
        at[0] = 0
        m_lo = carve(ring, NT)
        m_val = carve(ring, NT)
        m_col = carve(ring, NT, I32)
        m_code = ring[:, at[0]:at[0] + NT].bitcast(I32)
        msg = carve(ring, 2 * T * D).rearrange("p (s d) -> p s d", d=D)
        onehot = carve(ring, SR * BUCKET).rearrange("p (s r) -> p s r", r=BUCKET)
        assert at[0] <= 2 * L * D
        at[0] = 0
        nh1 = carve(big, L * P)
        xT = carve(big, 2 * LG * P).rearrange("p (s n) -> p s n", s=2)
        ysum = carve(big, 2 * LG * P).rearrange("p (s n) -> p s n", s=2)
        nh2 = carve(big, 2 * LG * P).rearrange("p (s n) -> p s n", s=2)
        hsum = carve(big, 4 * D).rearrange("p (s d) -> p s d", s=4)
        hrow = carve(big, D)
        hsT = carve(big, P)
        bias2 = carve(big, P)
        beta = carve(big, L)
        sess = carve(big, 4 * D).rearrange("p (s d) -> p s d", s=4)
        selT = carve(big, P)
        junk = carve(big, D)
        rown = carve(big, 8)
        normed = carve(big, NR * 2 * D).rearrange("p (s q d) -> p s q d", s=NR, q=2)
        assert at[0] <= ROWS
        seq = ring[:, :].rearrange("p (h l d) -> p h l d", h=2, l=L)

        stage = sb("stage", [P, 4 * 512 * 2])
        ostage = stage[:, :].rearrange("p (s n) -> p s n", s=4)
        gnr = sb("gnr", [P, 2, 2, D])
        ident = sb("ident", [P, P])
        ones = sb("ones", [P, P])
        onesb = sb("onesb", [P, P], BF16)
        lower = sb("lower", [P, P], BF16)
        iota_r = sb("iota_r", [P, BUCKET])
        iota_bc = sb("iota_bc", [P, NB, C], BF16)
        iota_l = sb("iota_l", [P, L])
        gate = sb("gate", [P, 3])
        toti = sb("toti", [P, NB], I32)
        toti2 = sb("toti2", [P, NB], I32)
        sqj = sb("sqj", [P, 2, D])
        tot = sb("tot", [P, NB])
        ginv2 = sb("ginv2", [P, 2 * NB])
        ntile = sb("ntile", [P, NB])
        cum = sb("cum", [P, NB])
        start = sb("start", [P, NB])
        picked = sb("picked", [P, NB])
        at[0] = 0
        counts = [carve(stage, GR * NB, dt).rearrange("p (g b) -> p g b", b=NB) for dt in (F32, I32, F32, F32)]
        gcnt, gpad_i, gpad, gcum = counts
        lstart = sb("lstart", [P, GR + 1, NB + 1])
        lscol = sb("lscol", [NB + 1, GR])
        dscol = sb("dscol", [NB + 1, GR])
        dsnow = sb("dsnow", [NB + 1, 1])
        block_id = sb("block_id", [P, NK])
        block_to = sb("block_to", [P, NK], I32)
        iota_p = sb("iota_p", [P, P], BF16)
        moved = sb("moved", [P, LC, 2])
        mlo = sb("mlo", [P, 2 * T])
        mval = sb("mval", [P, 2 * T])
        cring = sb("cring", [P, 2 * T], I32)
        startc = sb("startc", [P, 1])
        tile_off = sb("tile_off", [1, NT], I32)
        base = sb("base", [P, 2, NB])
        oh = sb("oh", [P, 2, NB, C], BF16)
        posf = sb("posf", [P, C])
        posi = sb("posi", [P, C], I32)
        place_i = sb("place_i", [P, 3, C], I32)
        place_p = sb("place_p", [P, 2, C], BF16)
        place_c = sb("place_c", [P, 2, C], BF16)
        idle = sb("idle", [P, Q])
        it_i = sb("it_i", [P, BT, L], I32)
        al_i = sb("al_i", [P, BT, L], I32)
        in_i = sb("in_i", [P, BT, L], I32)
        it_f = sb("it_f", [P, BT, L])
        it_n = sb("it_n", [P, BT, L])
        al_f = sb("al_f", [P, BT, L])
        mask = sb("mask", [P, BT, L])
        maskn = sb("maskn", [P, BT, L])
        mcnt = sb("mcnt", [P, BT])
        mrec = sb("mrec", [P, BT])
        sidf = sb("sidf", [P, L, BT])
        sidi = sb("sidi", [P, L, BT], I32)
        junkl = sb("junkl", [P, BT, L])
        ssq = sb("ssq", [P, 2 * NB])
        ginv = sb("ginv", [P, 2 * NB])
        w1a = sb("w1a", [D, D])
        w1b = sb("w1b", [D, D])
        w2c = sb("w2c", [D, 1])
        g1 = sb("g1", [D, D])
        g2 = sb("g2", [D, D])
        g1T = sb("g1T", [D, D])
        g2T = sb("g2T", [D, D])
        b1c = sb("b1c", [D, 1])
        erow = sb("erow", [L, D])
        eT = sb("eT", [D, L])
        posb = sb("posb", [D, L])

        bank = [ctx.enter_context(nc.psum_tensor(f"bank{i}", [P, 512], F32)) for i in range(8)]

        def in_bank(bt, k, q):
            return bank[q + (2 * (k % 2) if bt == 0 else 0)]

        def octv(b):
            return bank[b][:, 0:NB * C].rearrange("p (b t) -> p b t", t=C)

        s_edge = sem("s_edge")
        s_sess = sem("s_sess")
        s_wts = sem("s_wts")
        s_cst = sem("s_cst")
        s_gate = sem("s_gate")
        s_init = sem("s_init")
        s_zero = sem("s_zero")
        s_v = sem("s_v")
        s_oh1 = sem("s_oh1")
        s_h = sem("s_h")
        s_red = sem("s_red")
        s_ls = sem("s_ls")
        s_lc = sem("s_lc")
        s_lcc = sem("s_lcc")
        s_tge = sem("s_tge")
        s_toff = sem("s_toff")
        s_oh = sem("s_oh")
        s_base = sem("s_base")
        s_rank = sem("s_rank")
        s_rel = sem("s_rel")
        s_hc = sem("s_hc")
        s_hp = sem("s_hp")
        s_val = sem("s_val")
        s_pm = sem("s_pm")
        s_bg = sem("s_bg")
        s_dst = sem("s_dst")
        s_to = sem("s_to")
        s_gev = sem("s_gev")
        s_sct = sem("s_sct")
        s_free = sem("s_free")
        s_mtr = sem("s_mtr")
        s_mtc = sem("s_mtc")
        s_mta = sem("s_mta")
        s_meta = sem("s_meta")
        s_mr = sem("s_mr")
        s_g = [sem(f"s_g{u}") for u in range(2 * T)]
        s_S = sem("s_S")
        s_mm = sem("s_mm")
        s_acc = sem("s_acc")
        s_t1 = sem("s_t1")
        s_t1a = sem("s_t1a")
        s_t1v = sem("s_t1v")
        s_t1w = sem("s_t1w")
        s_eld = sem("s_eld")
        s_fld = sem("s_fld")
        s_fz = sem("s_fz")
        s_ec = sem("s_ec")
        s_eT = sem("s_eT")
        s_ea = sem("s_ea")
        s_t2 = sem("s_t2")
        s_g2r = sem("s_g2r")
        s_ssq = sem("s_ssq")
        s_cmb = sem("s_cmb")
        s_cw = sem("s_cw")
        s_wT = sem("s_wT")
        s_wTc = sem("s_wTc")
        s_pos = sem("s_pos")
        s_posc = sem("s_posc")
        s_sqv = sem("s_sqv")
        s_nrm = sem("s_nrm")
        s_gi = sem("s_gi")
        s_gn = sem("s_gn")
        s_gnT = sem("s_gnT")
        s_gnc = sem("s_gnc")
        s_sid = sem("s_sid")
        s_sq = s_g[0:2 * NG]
        s_x = sem("s_x")
        s_xc = sem("s_xc")
        s_hs = sem("s_hs")
        s_hT = sem("s_hT")
        s_z = sem("s_z")
        s_th = sem("s_th")
        s_hsc = sem("s_hsc")
        s_p2 = sem("s_p2")
        s_b2 = sem("s_b2")
        s_y = sem("s_y")
        s_ya = sem("s_ya")
        s_sg = sem("s_sg")
        s_bt = sem("s_bt")
        s_bm = sem("s_bm")
        s_ss = sem("s_ss")
        s_sn = sem("s_sn")
        s_sT = sem("s_sT")
        s_sTc = sem("s_sTc")
        s_sc = sem("s_sc")
        s_sca = sem("s_sca")
        s_scv = sem("s_scv")
        s_out = [sem(f"s_out{i}") for i in range(4)]

        block = ctx.enter_context(nc.Block())
        GRP = 7
        assert NB % GRP == 0
        emb_full = N // P
        emb_rest = N - emb_full * P
        tab = [t.rearrange("(g p) d -> p g d", p=P) for t in (table1, combined)]
        big_rows = big[:, :].rearrange("p (g d) -> p g d", d=D)
        acc_rows = acc[:, :].rearrange("p (g d) -> p g d", d=D)
        ring_rows = ring[:, 0:ROWS].rearrange("p (g d) -> p g d", d=D)

        @block.sync
        def _(sp):
            sp.wait_ge(s_init, 3)
            for n, (dst, src) in enumerate(((e_row, adj_row), (e_col, adj_col), (e_val, adj_val))):
                sp.dma_start(dst[:, 0:COLS], src[0:COLS * P].rearrange("(p t) -> p t", t=COLS)).then_inc(s_edge, 16)
                sp.dma_start(dst[0:TAIL, COLS:COLS + 1],
                             src[COLS * P:E].rearrange("(p t) -> p t", t=1)).then_inc(s_edge, 16)
            sp.wait_ge(s_cst, 1)
            sp.dma_start(slots.rearrange("(p x) w -> p (x w)", p=P), acc[:, 0:NT * 2]).then_inc(s_zero, 16)
            sp.wait_ge(s_free, GR + 2)
            lines = slots.rearrange("(j x) w -> j (x w)", x=P // R)
            full = NT // P
            sp.dma_start(big[:, 0:full * 2 * P].rearrange("p (m w) -> p m w", m=full),
                         lines[0:full * P, :].rearrange("(m p) w -> p m w", p=P)).then_inc(s_meta, 16)
            sp.dma_start(big[0:NT - full * P, full * 2 * P:(full + 1) * 2 * P], lines[full * P:NT, :]
                         ).then_inc(s_meta, 16)
            for r in range(NB // GRP):
                sp.wait_ge(s_t1a, (GRP * (r + 1) + 1) // 2)
                sp.wait_ge(s_t1v, (GRP * (r + 1)) // 2)
                a, b = 2 * GRP * r, 2 * GRP * (r + 1)
                sp.dma_start(tab[0][:, a:b, :], big_rows[:, a:b, :]).then_inc(s_t1w, 16)
            sp.wait_ge(s_t1w, 16 * (NB // GRP))
            sp.dma_start(big_rows[:, 0:emb_full, :],
                         emb[0:emb_full * P, :].rearrange("(g p) d -> p g d", p=P)).then_inc(s_eld, 16)
            sp.wait_ge(s_fz, 1)
            sp.dma_start(big_rows[0:emb_rest, emb_full, :], emb[emb_full * P:N, :]).then_inc(s_eld, 16)
            sp.wait_ge(s_ec, NB)
            sp.dma_start(big_rows[0:emb_rest, emb_full, :], features[emb_full * P:N, :]).then_inc(s_fld, 16)
            sp.dma_start(big_rows[:, 0:emb_full, :],
                         features[0:emb_full * P, :].rearrange("(g p) d -> p g d", p=P)).then_inc(s_fld, 16)
            for r in range(NB // GRP):
                sp.wait_ge(s_cmb, GRP * (r + 1))
                a, b = 2 * GRP * r, 2 * GRP * (r + 1)
                sp.dma_start(tab[1][:, a:b, :], ring_rows[:, a:b, :]).then_inc(s_cw, 16)
            for bt in range(BT):
                for q in range(-(-NS // 2)):
                    m = (-(-NS // 2)) * bt + q
                    sp.wait_ge(s_sca, m + 1)
                    if 2 * q + 1 < NS:
                        sp.wait_ge(s_scv, (NS // 2) * bt + q + 1)
                    a, b = 1024 * q, min(1024 * q + 1024, N)
                    sp.dma_start(out[bt * P:(bt + 1) * P, a:b], ostage[:, m % 4, 0:b - a]).then_inc(s_out[m % 4], 16)
            total = (-(-NS // 2)) * BT
            for i in range(4):
                sp.wait_ge(s_out[i], 16 * ((total - i + 3) // 4))

        @block.gpsimd
        def _(pool):
            pool.memset(acc[:, :], 0.0).then_inc(s_cst, 1)
            pool.memset(gate[:, :], 0.0).then_inc(s_gate, 1)
            pool.memset(ones[:, :], 1.0).then_inc(s_cst, 1)
            pool.memset(ident[:, :], 0.0).then_inc(s_cst, 1)
            pool.memset(onesb[:, :], 1.0).then_inc(s_cst, 1)
            pool.iota(iota_r[:, :], [[1, BUCKET]], base=0, channel_multiplier=0,
                      allow_small_or_imprecise_dtypes=True).then_inc(s_cst, 1)
            pool.iota(iota_bc[:, :, :], [[1, NB], [0, C]], base=0, channel_multiplier=0,
                      allow_small_or_imprecise_dtypes=True).then_inc(s_cst, 1)
            pool.iota(iota_l[:, :], [[1, L]], base=0, channel_multiplier=0,
                      allow_small_or_imprecise_dtypes=True).then_inc(s_cst, 1)
            pool.iota(tile_iota[:, :], [[1, NT]], base=0, channel_multiplier=0,
                      allow_small_or_imprecise_dtypes=True).then_inc(s_cst, 1)
            pool.iota(iota_p[:, :], [[R, P]], base=0, channel_multiplier=0,
                      allow_small_or_imprecise_dtypes=True).then_inc(s_cst, 1)
            pool.iota(iota_c[:, :, :], [[1, LC], [0, C]], base=0, channel_multiplier=0,
                      allow_small_or_imprecise_dtypes=True).then_inc(s_cst, 1)
            pool.iota(block_at[:, :], [[R, NK * P]], base=0, channel_multiplier=0,
                      allow_small_or_imprecise_dtypes=True).then_inc(s_cst, 1)
            pool.iota(block_id[:, :], [[P, NK]], base=0, channel_multiplier=1,
                      allow_small_or_imprecise_dtypes=True).then_inc(s_cst, 1)
            pool.wait_ge(s_cst, 12)
            pool.affine_select(out=ident[:, :], in_=ident[:, :], compare_op=ALU.not_equal, fill=1.0, base=0,
                               pattern=[[-1, P]], channel_multiplier=1).then_inc(s_cst, 1)
            pool.affine_select(out=lower[:, :], in_=onesb[:, :], compare_op=ALU.is_gt, fill=0.0, base=0,
                               pattern=[[1, P]], channel_multiplier=-1).then_inc(s_cst, 1)

            def opened(n, waits):
                pool.wait_ge(s_gate, n + 1)
                for s, v in waits:
                    ge(pool, s, v)
                pool.tensor_tensor(gate[:, 0:1], gate[:, 1:2], gate[:, 1:2], ALU.add).then_inc(s_gate, 1)

            pool.sem_inc(s_free, 2)
            pool.wait_ge(s_zero, 16)
            with pool.Fori(0, GR) as g:
                opened(g, [(s_gev, g + 2), (s_to, g + 1)])
                for k in range(NK):
                    pool.indirect_dma_start(slots, bass.IndirectOffsetOnAxis(block_to[:, k:k + 1], 0),
                                            moved[:, k * R:(k + 1) * R, :].rearrange("p r w -> p (r w)"), None,
                                            bounds_check=NT * P // R - 1, oob_is_err=False).then_inc(s_sct, 16)
                pool.wait_ge(s_free, g + 2)
                pool.wait_ge(s_sct, 16 * NK * (g + 1))
                pool.tensor_tensor(gate[:, 2:3], gate[:, 1:2], gate[:, 1:2], ALU.add).then_inc(s_free, 1)

            def gather_step(layer, source, c, h):
                opened(GR + NST * layer + c, [(s_mr, NST * layer + c + 1)] +
                       ([(s_mm, NT * layer + T * (c - 1))] if not (isinstance(c, int) and c < 2) else []))
                for u in range(T):
                    s = h * T + u
                    pool.indirect_dma_start(msg[:, s, :], None, source,
                                            bass.IndirectOffsetOnAxis(cring[:, s:s + 1], 0)).then_inc(s_g[s], 16)

            for layer, source in enumerate((emb, table1)):
                if layer:
                    pool.wait_ge(s_t1w, 16 * (NB // GRP))
                for c in range(2):
                    gather_step(layer, source, c, c)
                with pool.Fori(1, NST // 2) as i:
                    for h in range(2):
                        gather_step(layer, source, 2 * i + h, h)

            pool.wait_ge(s_cw, 16 * (NB // GRP))
            pool.wait_ge(s_sid, 1)
            for bt in range(BT):
                half = bt % 2
                if bt >= 2:
                    pool.wait_ge(s_ss, bt - 1)
                for l in range(L):
                    pool.indirect_dma_start(seq[:, half, l, :], None, combined,
                                            bass.IndirectOffsetOnAxis(sidi[:, l, bt:bt + 1], 0)
                                            ).then_inc(s_sq[half * NG + l // LG], 16)

        @block.scalar
        def _(act):
            for dst, src in ((it_i, items), (al_i, alias), (in_i, inputs)):
                act.dma_start(dst[:, :, :], src.rearrange("(b p) l -> p b l", p=P)).then_inc(s_sess, 16)
            act.dma_start(w1a[:, :], w_1[0:D, :]).then_inc(s_wts, 16)
            act.dma_start(w1b[:, :], w_1[D:2 * D, :]).then_inc(s_wts, 16)
            act.dma_start(w2c[:, :], w_2).then_inc(s_wts, 16)
            act.dma_start(g1[:, :], glu1_w).then_inc(s_wts, 16)
            act.dma_start(g2[:, :], glu2_w).then_inc(s_wts, 16)
            act.dma_start(b1c[:, :], glu1_b.rearrange("(p o) -> p o", o=1)).then_inc(s_wts, 16)
            act.dma_start(erow[:, :], emb[0:L, :]).then_inc(s_wts, 16)
            act.wait_ge(s_wT, 3)
            act.copy(g1T[:, :], bank[5][:, 0:D]).then_inc(s_wTc, 1)
            act.copy(g2T[:, :], bank[5][:, D:2 * D]).then_inc(s_wTc, 1)
            act.copy(eT[:, :], bank[5][:, 2 * D:2 * D + L]).then_inc(s_wTc, 1)
            act.wait_ge(s_pos, 1)
            act.copy(posb[:, :], bank[6][:, 0:L]).then_inc(s_posc, 1)
            def evacuate():
                act.copy(moved[:, :, :].rearrange("p c w -> p w c"),
                         bank[4][:, 0:2 * LC].rearrange("p (w c) -> p w c", w=2)).then_inc(s_gev, 1)

            act.wait_ge(s_init, 5)
            with act.Fori(0, GR) as g:
                for s in range(SG):
                    n, r = SG * g + s, s % Q
                    act.wait_ge(s_hc, n + 2)
                    act.wait_ge(s_pm, n + 1)
                    act.copy(idle[:, r:r + 1], ones[:, 0:1])
                    for t in range(C):
                        if s == 1 and t == C // 2:
                            act.wait_ge(s_pm, SG * g + 4)
                            act.wait_ge(s_free, g + 1)
                            evacuate()
                        for q, what in enumerate((code, e_val)):
                            last = act.activation(at_c[:, r, t, q, :], hot_c[:, r, :, t], ACT.Copy,
                                                  scale=what[:, bass.ds(n * C + t, 1)])
                        last.then_inc(s_val, 1)
            act.wait_ge(s_pm, SG * GR + 4)
            act.wait_ge(s_free, GR + 1)
            evacuate()
            for m in range(-(-NT // P)):
                w = min(P, NT - P * m)
                act.wait_ge(s_mtr, m + 1)
                act.copy(m_val[:, m * P:m * P + w], bank[2 + m % 2][:, 0:w]).then_inc(s_mta, 1)
            for g in range(0, NB, 2):
                act.wait_ge(s_t1, g + 1)
                act.copy(big[:, 2 * D * g:2 * D * (g + 1)], bank[5][:, 0:2 * D]).then_inc(s_t1a, 1)
            act.wait_ge(s_eld, 32)

            def emb_rows(c, h):
                act.wait_ge(s_eT, c + 1)
                act.copy(idle[:, h:h + 1], ones[:, 0:1])
                act.copy(gnr[:, h, :, :], big_rows[:, bass.ds(2 * c, 2), :]).then_inc(s_ec, 1)

            with act.Fori(0, LOOP // 2) as i:
                for h in range(2):
                    emb_rows(2 * i + h, h)
            for c in range(LOOP, NB):
                emb_rows(c, c % 2)
            for g in range(NB):
                act.wait_ge(s_t2, g + 1)
                act.copy(acc[:, 2 * D * g:2 * D * (g + 1)], bank[5 + g % 2][:, 0:2 * D]).then_inc(s_g2r, 1)
            act.wait_ge(s_g2r, NB)
            for g in range(0, NB, 2):
                for q in range(2):
                    ge(act, s_ssq, g + q - 1)
                    act.activation(sqj[:, q, :], acc[:, (2 * g + q) * D:(2 * g + q + 1) * D], ACT.Square,
                                   scale=1.0 / (LAYERS + 1), accum_out=ssq[:, 2 * g + q:2 * g + q + 1]
                                   ).then_inc(s_ssq, 1)
            act.wait_ge(s_ssq, 2 * ((NB + 1) // 2))
            act.wait_ge(s_sqv, 1)
            act.activation(ginv[:, :], ssq[:, :], ACT.Sqrt).then_inc(s_nrm, 1)
            act.wait_ge(s_gi, 3)
            for g in range(NB):
                ge(act, s_gnT, g - NR + 1)
                for q in range(2):
                    last = act.activation(normed[:, g % NR, q, :], acc[:, (2 * g + q) * D:(2 * g + q + 1) * D], ACT.Copy,
                                          scale=ginv2[:, 2 * g + q:2 * g + q + 1])
                last.then_inc(s_gn, 1)

            def tanh_step(bt, k):
                m, w = NG * bt + k, min(LG, L - LG * k)
                act.wait_ge(s_z, m + 1)
                ge(act, s_y, NG * (bt - 1) + k + 1)
                for j in range(w):
                    l = LG * k + j
                    last = act.activation(nh1[:, l * P:(l + 1) * P], in_bank(bt, k, 1)[:, j * P:(j + 1) * P],
                                          ACT.Tanh, bias=posb[:, L - 1 - l:L - l])
                last.then_inc(s_th, 1)

            def read_in(bt, k):
                if bt >= BT:
                    return
                m, w = NG * bt + k, min(LG, L - LG * k)
                if k < NG:
                    act.wait_ge(s_x, m + 1)
                    ge(act, s_z, m - 1)
                    act.copy(xT[:, m % 2, 0:w * P], in_bank(bt, k, 0)[:, 0:w * P]).then_inc(s_xc, 1)
                if k:
                    tanh_step(bt, k - 1)

            for k in range(NG + 1):
                read_in(0, k)
            for w in range(BT + 1):
                for k in range(NG):
                    if w < BT:
                        m, n = NG * w + k, min(LG, L - LG * k) * P
                        act.wait_ge(s_ya, m + 1)
                        ge(act, s_bt, m - 1)
                        act.activation(nh2[:, m % 2, 0:n], ysum[:, m % 2, 0:n], ACT.Sigmoid).then_inc(s_sg, 1)
                    read_in(w + 1, k)
                    if w and 2 * k < NS:
                        m = (-(-NS // 2)) * (w - 1) + k
                        n = 512 if 2 * k < NS - 1 else REM
                        act.wait_ge(s_sc, NS * (w - 1) + 2 * k + 1)
                        ge(act, s_out[m % 4], 16 * (m // 4))
                        act.copy(ostage[:, m % 4, 0:n], bank[5][:, 0:n]).then_inc(s_sca, 1)
                read_in(w + 1, NG)
                if w < BT:
                    act.wait_ge(s_sn, 5 * w + 1)
                    act.activation(rown[:, 1:2], rown[:, 0:1], ACT.Sqrt).then_inc(s_sn, 1)

        @block.vector
        def _(dve):
            dve.memset(e_row[:, COLS:ECOLS], -1).then_inc(s_init, 1)
            dve.memset(e_col[:, COLS:ECOLS], 0).then_inc(s_init, 1)
            dve.memset(e_val[:, COLS:ECOLS], 0.0).then_inc(s_init, 1)
            dve.memset(lstart[:, GR, :], 0.0).then_inc(s_init, 1)
            dve.memset(place_p[:, 1, :], 0.0)
            dve.memset(at_p[:, 2, :, :], 0.0)
            dve.memset(place_c[:, 1, :], 0.0).then_inc(s_init, 1)
            chain = [0]

            def link(ins):
                chain[0] += 1
                ins.then_inc(s_v, 1)
                dve.wait_ge(s_v, chain[0])

            dve.wait_ge(s_edge, 96)
            dve.wait_ge(s_init, 5)
            link(dve.tensor_single_scalar(bkt_i, e_row, BUCKET.bit_length() - 1, ALU.arith_shift_right))
            link(dve.tensor_copy(bkt, bkt_i))
            dve.sem_inc(s_red, 1)
            dve.wait_ge(s_cst, 14)

            def count_step(n, q):
                dve.wait_ge(s_h, n + 1)
                dve.tensor_tensor(oh1[:, q, :, :], iota_bc[:, :, :],
                                  bkt[:, bass.ds(n * C, C)].unsqueeze(1).broadcast_to([P, NB, C]),
                                  ALU.is_equal).then_inc(s_oh1, 1)

            for q in range(Q):
                count_step(q, q)
            with dve.Fori(0, GR) as g:
                for s in range(SG):
                    count_step(SG * g + s + Q, s % Q)
                dve.wait_ge(s_h, SG * (g + 1) + Q)
                dve.tensor_copy(gcnt[:, bass.ds(g, 1), :], bank[4][:, 0:NB].unsqueeze(1)).then_inc(s_red, 1)
            dve.wait_ge(s_red, GR + 1)
            link(dve.tensor_scalar(gpad_i[:, :, :], gcnt[:, :, :], float(R - 1), None, ALU.add))
            link(dve.tensor_single_scalar(gpad_i[:, :, :], gpad_i[:, :, :], -R, ALU.bitwise_and))
            link(dve.tensor_copy(gpad[:, :, :], gpad_i[:, :, :]))
            for g in range(GR):
                last = dve.tensor_tensor_scan(gcum[:, g, :], ones[:, 0:NB], gpad[:, g, :], 0.0, ALU.mult, ALU.add)
            link(last)
            dve.tensor_copy(lstart[:, 0:GR, NB:NB + 1], gcum[:, :, NB - 1:NB])
            link(dve.tensor_tensor(lstart[:, 0:GR, 0:NB], gcum[:, :, :], gpad[:, :, :], ALU.subtract))
            link(dve.tensor_reduce(tot[:, :], gpad[:, :, :].rearrange("p g b -> p b g"), AX_X, ALU.add))
            link(dve.tensor_scalar(toti[:, :], tot[:, :], float(P - 1), None, ALU.add))
            link(dve.tensor_single_scalar(toti2[:, :], toti[:, :], P.bit_length() - 1, ALU.arith_shift_right))
            link(dve.tensor_copy(ntile[:, :], toti2[:, :]))
            link(dve.tensor_tensor_scan(cum[:, :], ones[:, 0:NB], ntile[:, :], 0.0, ALU.mult, ALU.add))
            link(dve.tensor_tensor(start[:, :], cum[:, :], ntile[:, :], ALU.subtract))
            link(dve.tensor_scalar(gofs[:, 0, :], start[:, :], float(P), None, ALU.mult))
            for g in range(1, GR):
                link(dve.tensor_tensor(gofs[:, g, :], gofs[:, g - 1, :], gpad[:, g - 1, :], ALU.add))
            dve.memset(delta[:, :, NB:NB + 1], FAR)
            link(dve.tensor_tensor(delta[:, :, 0:NB], gofs[:, :, :], lstart[:, 0:GR, 0:NB], ALU.subtract))
            link(dve.tensor_scalar(delta[:, :, :], delta[:, :, :], 1.0 / R, None, ALU.mult))
            dve.tensor_copy(dstep[:, :, 0:1], delta[:, :, 0:1])
            dve.tensor_tensor(dstep[:, :, 1:NB + 1], delta[:, :, 1:NB + 1], delta[:, :, 0:NB], ALU.subtract).then_inc(s_ls, 1)
            link(dve.tensor_tensor_reduce(picked[0:NB, :], start[0:NB, :], ident[0:NB, 0:NB], 1.0, 0.0,
                                          ALU.mult, ALU.add, startc[0:NB, :]))
            dve.tensor_scalar(tile_ge[0:NB, :], tile_iota[0:NB, :], startc[0:NB, 0:1], None, ALU.is_ge).then_inc(s_tge, 1)
            dve.wait_ge(s_lc, 1)
            dve.tensor_copy(lscol[:, :], bank[5][0:NB + 1, 0:GR])
            dve.tensor_copy(dscol[:, :], bank[5][0:NB + 1, GR:2 * GR]).then_inc(s_lcc, 1)
            dve.wait_ge(s_tge, 2)
            for n in range(3):
                a, b = n * TW, min(NT, (n + 1) * TW)
                dve.tensor_scalar(tile_off[0:1, a:b], bank[5 + n][0:1, 0:b - a], -1.0, float(BUCKET),
                                  ALU.add, ALU.mult).then_inc(s_toff, 1)
            link(dve.tensor_single_scalar(bkt_i, e_row, BUCKET - 1, ALU.bitwise_and))
            link(dve.tensor_scalar(col_f, e_col, 0.0, float(N - 1), ALU.max, ALU.min))
            link(dve.scalar_tensor_tensor(code, col_f, float(BUCKET), bkt_i, ALU.mult, ALU.add))
            link(dve.scalar_tensor_tensor(code, bkt, 0.0, code, ALU.is_ge, ALU.mult))
            dve.memset(at_c[:, 2:4, :, :, :], 0.0).then_inc(s_init, 1)
            def build(n, h):
                dve.tensor_tensor(oh[:, h, :, :], iota_bc[:, :, :],
                                  bkt[:, bass.ds(n * C, C)].unsqueeze(1).broadcast_to([P, NB, C]),
                                  ALU.is_equal).then_inc(s_oh, 1)

            def hot_columns(n, r):
                dve.wait_ge(s_val, C * n + 1)
                dve.tensor_tensor(hot_c[:, r, :, :], iota_c[:, :, :],
                                  place_c[:, r % 2, :].unsqueeze(1).broadcast_to([P, LC, C]), ALU.is_equal).then_inc(s_hc, 1)

            def hot_partitions(n, r, part):
                t = slice(part * C // 2, (part + 1) * C // 2)
                if part == 0:
                    dve.wait_ge(s_pm, n + 1)
                dve.tensor_tensor(at_p[:, r, t, :], iota_p[:, :].unsqueeze(1).broadcast_to([P, C // 2, P]),
                                  place_p[:, r % 2, t].unsqueeze(2).broadcast_to([P, C // 2, P]),
                                  ALU.is_equal).then_inc(s_hp, 1)

            def sort_step(g, s, v):
                n, h = SG * g + s, s % 2
                dve.wait_ge(s_rank, n + 1)
                if s < SG - 1:
                    dve.tensor_tensor(base[:, 1 - h, :], base[:, h, :], bank[2 + h][:, 0:NB], ALU.add).then_inc(s_base, 1)
                else:
                    dve.tensor_copy(base[:, 1 - h, :], lstart[:, bass.ds(g + 1, 1), 0:NB].rearrange("p o b -> p (o b)")
                                    ).then_inc(s_base, 1)
                dve.tensor_tensor(rank[:, :, :], octv(h), oh[:, h, :, :], ALU.mult).then_inc(s_rel, 1)
                dve.wait_ge(s_v, v)
                hot_columns(n, (s - 1) % Q)
                dve.wait_ge(s_rel, n + 3)
                dve.tensor_reduce(posf[:, :], rank[:, :, :].rearrange("p b t -> p t b"), AX_X, ALU.add).then_inc(s_v, 1)
                hot_partitions(n, (s - 1) % Q, 0)
                dve.wait_ge(s_v, v + 1)
                dve.tensor_copy(posi[:, :], posf[:, :]).then_inc(s_v, 1)
                hot_partitions(n, (s - 1) % Q, 1)
                dve.wait_ge(s_v, v + 2)
                dve.tensor_single_scalar(place_i[:, 0, :], posi[:, :], (P - 1) * R, ALU.bitwise_and)
                dve.tensor_scalar(place_i[:, 1, :], posi[:, :], P.bit_length() - 1, -R,
                                  ALU.arith_shift_right, ALU.bitwise_and)
                dve.tensor_single_scalar(place_i[:, 2, :], posi[:, :], R - 1, ALU.bitwise_and).then_inc(s_v, 1)
                build(n + 2, h)
                dve.wait_ge(s_v, v + 3)
                dve.tensor_copy(place_p[:, h, :], place_i[:, 0, :])
                dve.tensor_tensor(place_c[:, h, :], place_i[:, 1, :], place_i[:, 2, :], ALU.add).then_inc(s_v, 1)

            def targets(g, part):
                if part == 0:
                    dve.tensor_copy(dsnow[:, :], dscol[:, bass.ds(g, 1)])
                    dve.tensor_scalar(begun[0:NB + 1, :], block_at[0:NB + 1, :], lscol[:, bass.ds(g, 1)], None,
                                      ALU.is_ge).then_inc(s_bg, 1)
                else:
                    dve.wait_ge(s_dst, g + 1)
                    dve.wait_ge(s_free, g + 2)
                    dve.tensor_tensor(block_to[:, :], bank[7][:, 0:NK], block_id[:, :], ALU.add).then_inc(s_to, 1)

            v0 = chain[0]
            dve.wait_ge(s_lcc, 1)
            dve.sem_inc(s_rel, 2)
            dve.tensor_copy(base[:, 0, :], lstart[:, 0, 0:NB]).then_inc(s_base, 1)
            build(0, 0)
            build(1, 1)
            dve.sem_inc(s_val, Q * C + 1)
            dve.sem_inc(s_hp, 2)
            with dve.Fori(0, GR) as g:
                for s in range(SG):
                    sort_step(g, s, v0 + 4 * (SG * g + s))
                    if s == 1:
                        targets(g, 0)
                    if s == SG - 1:
                        targets(g, 1)
            chain[0] = v0 + 4 * SG * GR
            dve.wait_ge(s_v, chain[0])
            hot_columns(SG * GR, Q - 1)
            hot_partitions(SG * GR, Q - 1, 0)
            hot_partitions(SG * GR, Q - 1, 1)
            for m in range(-(-NT // P)):
                w = min(P, NT - P * m)
                dve.wait_ge(s_mtr, m + 1)
                dve.tensor_copy(m_code[:, m * P:m * P + w], bank[m % 2][:, 0:w]).then_inc(s_mtc, 1)
            dve.wait_ge(s_mtc, -(-NT // P))
            dve.tensor_single_scalar(m_col, m_code, BUCKET.bit_length() - 1, ALU.arith_shift_right)
            link(dve.tensor_single_scalar(m_code, m_code, BUCKET - 1, ALU.bitwise_and))
            link(dve.tensor_copy(m_lo, m_code))
            dve.wait_ge(s_mta, -(-NT // P))

            def fetch(c, h, layer):
                dve.tensor_copy(mlo[:, h * T:(h + 1) * T], m_lo[:, bass.ds(c * T, T)])
                dve.tensor_copy(mval[:, h * T:(h + 1) * T], m_val[:, bass.ds(c * T, T)])
                dve.tensor_copy(cring[:, h * T:(h + 1) * T], m_col[:, bass.ds(c * T, T)]).then_inc(s_mr, 1)

            def one_hot(u):
                dve.tensor_scalar(onehot[:, u % SR, :], iota_r[:, :], mlo[:, u:u + 1], mval[:, u:u + 1],
                                  ALU.is_equal, ALU.mult).then_inc(s_S, 1)

            def session_inputs():
                dve.wait_ge(s_sess, 48)
                dve.tensor_copy(al_f[:, :, :], al_i[:, :, :])
                link(dve.tensor_copy(it_f[:, :, :], it_i[:, :, :]))
                link(dve.tensor_scalar(it_n[:, :, :], it_f[:, :, :], 0.0, float(N), ALU.is_lt, ALU.mult))
                link(dve.tensor_tensor(it_f[:, :, :], it_f[:, :, :], it_n[:, :, :], ALU.add))
                link(dve.tensor_scalar(it_n[:, :, :], it_f[:, :, :], 0.0, float(N - 1), ALU.max, ALU.min))
                link(dve.tensor_scalar(mask[:, :, :], in_i[:, :, :], 0.0, None, ALU.not_equal))
                link(dve.tensor_reduce(mcnt[:, :], mask[:, :, :], AX_X, ALU.add))
                link(dve.reciprocal(mrec[:, :], mcnt[:, :]))
                for bt in range(BT):
                    link(dve.tensor_scalar(maskn[:, bt, :], mask[:, bt, :], mrec[:, bt:bt + 1], None, ALU.mult))

            def session_rows(l, v):
                dve.wait_ge(s_v, v + l)
                for bt in range(BT):
                    last = dve.scalar_tensor_tensor(junkl[:, bt, :], iota_l[:, :], al_f[:, bt, bass.ds(l, 1)],
                                                    it_n[:, bt, :], ALU.is_equal, ALU.mult,
                                                    accum_out=sidf[:, bass.ds(l, 1), bt])
                last.then_inc(s_v, 1)

            def add_embeddings(c, h):
                dve.wait_ge(s_eT, c + 3)
                dve.wait_ge(s_acc, NT + T * (c + 1) + 1)
                dve.tensor_tensor(acc[:, bass.ds(2 * D * c, 2 * D)], acc[:, bass.ds(2 * D * c, 2 * D)],
                                  bank[5 + h][:, 0:2 * D], ALU.add).then_inc(s_ea, 1)

            def round_step(layer, c, h, last=False):
                if not last:
                    fetch(c + 1, 1 - h, layer)
                for u in range(T):
                    j = NT * layer + T * c + u
                    dve.wait_ge(s_mm, j + 1)
                    if not last or u + SR < T:
                        if u + SR == T:
                            dve.wait_ge(s_mr, NST * layer + c + 2)
                        one_hot((h * T + u + SR) % (2 * T))
                    off = dve.value_load(tile_off[0:1, bass.ds(T * c + u, 1)], min_val=0, max_val=ROWS - BUCKET)
                    dve.wait_ge(s_acc, j + 1)
                    if layer and u == 0:
                        dve.wait_ge(s_ea, c + 2 if not isinstance(c, int) else min(c, NB) + 2)
                    dve.tensor_tensor(acc[:, bass.ds(off, BUCKET)], acc[:, bass.ds(off, BUCKET)],
                                      bank[u % PR][:, 0:BUCKET], ALU.add).then_inc(s_acc, 1)
                if layer == 0 and not (isinstance(c, int) and c >= L):
                    session_rows(c, v1)
                if layer == 1 and not (isinstance(c, int) and c >= NB):
                    add_embeddings(c, h)

            dve.sem_inc(s_acc, 1)
            dve.wait_ge(s_zero, 16)
            for layer in range(LAYERS):
                if layer:
                    dve.wait_ge(s_mm, NT)
                fetch(0, 0, layer)
                dve.wait_ge(s_mr, NST * layer + 1)
                for u in range(SR):
                    one_hot(u)
                if layer == 0:
                    session_inputs()
                    v1 = chain[0]
                else:
                    dve.sem_inc(s_ea, 2)
                with dve.Fori(0, LOOP // 2) as i:
                    for h in range(2):
                        round_step(layer, 2 * i + h, h)
                for c in range(LOOP, NST):
                    round_step(layer, c, c % 2, last=(c == NST - 1))
                if layer == 0:
                    chain[0] += L
                    dve.wait_ge(s_v, chain[0])
                    dve.tensor_copy(sidi[:, :, :], sidf[:, :, :]).then_inc(s_sid, 1)
                    for g in range(1, NB, 2):
                        dve.wait_ge(s_t1, g + 1)
                        dve.tensor_copy(big[:, 2 * D * g:2 * D * (g + 1)], bank[6][:, 0:2 * D]).then_inc(s_t1v, 1)
                    dve.wait_ge(s_t1w, 16 * (NB // GRP))
                    dve.memset(big_rows[:, emb_full, :], 0.0).then_inc(s_fz, 1)

            dve.wait_ge(s_fld, 32)
            dve.wait_ge(s_mm, LAYERS * NT)
            for g in range(NB):
                cols = slice(2 * D * g, 2 * D * (g + 1))
                dve.wait_ge(s_g2r, g + 1)
                dve.scalar_tensor_tensor(ring[:, cols], acc[:, cols], 1.0 / (LAYERS + 1), big[:, cols],
                                         ALU.mult, ALU.add).then_inc(s_cmb, 1)
            v2 = chain[0]
            dve.wait_ge(s_cmb, NB)
            for n in range(2 * (NB // 2)):
                g = 2 * (n // 2) + 1
                cols = slice((2 * g + n % 2) * D, (2 * g + n % 2 + 1) * D)
                ge(dve, s_v, v2 + n - 3)
                last = dve.tensor_tensor_reduce(hsum[:, n % 4, :], acc[:, cols], acc[:, cols],
                                                1.0 / (LAYERS + 1) ** 2, 0.0, ALU.mult, ALU.add,
                                                ssq[:, 2 * g + n % 2:2 * g + n % 2 + 1]).then_inc(s_v, 1)
                chain[0] += 1
            dve.wait_ge(s_v, chain[0])
            dve.sem_inc(s_sqv, 1)
            dve.wait_ge(s_nrm, 1)
            dve.tensor_scalar(ginv[:, :], ginv[:, :], EPS, None, ALU.max).then_inc(s_gi, 1)
            dve.wait_ge(s_gi, 1)
            dve.reciprocal(ginv[:, :], ginv[:, :]).then_inc(s_gi, 1)
            dve.wait_ge(s_gi, 2)
            dve.tensor_scalar(ginv2[:, :], ginv[:, :], 1.0 / (LAYERS + 1), None, ALU.mult).then_inc(s_gi, 1)
            for g in range(NB):
                dve.wait_ge(s_gnT, g + 1)
                dve.tensor_copy(acc[:, 2 * D * g:2 * D * (g + 1)], bank[5 + g % 2][:, 0:2 * D]).then_inc(s_gnc, 1)
            dve.wait_ge(s_cw, 16 * (NB // GRP))

            def read_in(bt, k):
                if bt >= BT or k == NG:
                    return
                dve.wait_ge(s_sq[bt % 2 * NG + k], 16 * (NST + min(LG, L - LG * k) * (bt // 2 + 1)))
                dve.wait_ge(s_v, chain[0])
                for l in range(LG * k, min(L, LG * k + LG)):
                    if l >= 2:
                        dve.wait_ge(s_v, h_at[l - 2])
                        last = dve.scalar_tensor_tensor(hsum[:, l % 4, :], seq[:, bt % 2, l, :],
                                                        maskn[:, bt, l:l + 1], hsum[:, (l - 2) % 4, :],
                                                        ALU.mult, ALU.add)
                    else:
                        last = dve.tensor_scalar(hsum[:, l, :], seq[:, bt % 2, l, :], maskn[:, bt, l:l + 1],
                                                 None, ALU.mult)
                    last.then_inc(s_v, 1)
                    chain[0] += 1
                    h_at[l] = chain[0]
                if k == NG - 1:
                    dve.wait_ge(s_v, chain[0])
                    if bt:
                        dve.wait_ge(s_hT, bt)
                    dve.tensor_tensor(hrow[:, :], hsum[:, (L - 1) % 4, :], hsum[:, (L - 2) % 4, :],
                                      ALU.add).then_inc(s_hs, 1)

            def weigh(bt, k):
                m, w = NG * bt + k, min(LG, L - LG * k)
                dve.wait_ge(s_bt, m + 1)
                dve.tensor_tensor(beta[:, LG * k:LG * k + w], bank[(4, 7)[m % 2]][:, 0:w],
                                  mask[:, bt, LG * k:LG * k + w], ALU.mult).then_inc(s_bm, 1)
                dve.wait_ge(s_bm, m + 1)
                for l in range(LG * k, LG * k + w):
                    if l >= 2:
                        dve.wait_ge(s_v, e_at[l - 2])
                        last = dve.scalar_tensor_tensor(sess[:, l % 4, :], seq[:, bt % 2, l, :], beta[:, l:l + 1],
                                                        sess[:, (l - 2) % 4, :], ALU.mult, ALU.add)
                    else:
                        last = dve.tensor_scalar(sess[:, l, :], seq[:, bt % 2, l, :], beta[:, l:l + 1], None, ALU.mult)
                    last.then_inc(s_v, 1)
                    chain[0] += 1
                    e_at[l] = chain[0]

            h_at, e_at = {}, {}
            for k in range(NG):
                read_in(0, k)
            for w in range(BT + 1):
                if w < BT:
                    dve.wait_ge(s_hT, w + 1)
                    dve.tensor_copy(hsT[:, :], bank[4][:, P:2 * P]).then_inc(s_hsc, 1)
                    dve.wait_ge(s_p2, w + 1)
                    dve.tensor_scalar(bias2[:, :], bank[7][:, P:2 * P], b1c[:, 0:1], None, ALU.add).then_inc(s_b2, 1)
                    dve.wait_ge(s_b2, w + 1)
                for k in range(NG):
                    if w < BT:
                        m, n = NG * w + k, min(LG, L - LG * k)
                        dve.wait_ge(s_y, m + 1)
                        ge(dve, s_sg, m - 1)
                        dve.tensor_tensor(ysum[:, m % 2, 0:n * P].rearrange("p (l n) -> p l n", n=P),
                                          bank[2 + m % 2][:, 0:n * P].rearrange("p (l n) -> p l n", n=P),
                                          bias2[:, :].unsqueeze(1).broadcast_to([P, n, P]), ALU.add).then_inc(s_ya, 1)
                    if w and k == 0:
                        dve.wait_ge(s_sT, w)
                        dve.tensor_copy(selT[:, :], bank[4][:, 2 * P:3 * P]).then_inc(s_sTc, 1)
                    if w < BT and k:
                        weigh(w, k - 1)
                    read_in(w + 1, k)
                    if w and 2 * k + 1 < NS:
                        m = (-(-NS // 2)) * (w - 1) + k
                        dve.wait_ge(s_sc, NS * (w - 1) + 2 * k + 2)
                        ge(dve, s_out[m % 4], 16 * (m // 4))
                        dve.tensor_copy(ostage[:, m % 4, 512:1024], bank[6][:, :]).then_inc(s_scv, 1)
                if w < BT:
                    weigh(w, NG - 1)
                    dve.wait_ge(s_v, chain[0])
                    dve.tensor_tensor(junk[:, :], sess[:, (L - 1) % 4, :], sess[:, (L - 2) % 4, :], ALU.add).then_inc(s_ss, 1)
                    dve.wait_ge(s_ss, w + 1)
                    dve.tensor_tensor_reduce(sess[:, 0, :], junk[:, :], junk[:, :], 1.0, 0.0, ALU.mult, ALU.add,
                                             rown[:, 0:1]).then_inc(s_sn, 1)
                    dve.wait_ge(s_sn, 5 * w + 2)
                    dve.tensor_scalar(rown[:, 2:3], rown[:, 1:2], EPS, None, ALU.max).then_inc(s_sn, 1)
                    dve.wait_ge(s_sn, 5 * w + 3)
                    dve.reciprocal(rown[:, 3:4], rown[:, 2:3]).then_inc(s_sn, 1)
                    dve.wait_ge(s_sn, 5 * w + 4)
                    dve.tensor_scalar(sess[:, 1, :], junk[:, :], rown[:, 3:4], W_K, ALU.mult, ALU.mult).then_inc(s_sn, 1)

        @block.tensor
        def _(pe):
            pe.wait_ge(s_wts, 112)
            pe.wait_ge(s_cst, 14)
            pe.transpose(bank[5][:, 0:D], g1[:, :], ident[:, :]).then_inc(s_wT, 1)
            pe.transpose(bank[5][:, D:2 * D], g2[:, :], ident[:, :]).then_inc(s_wT, 1)
            pe.transpose(bank[5][:, 2 * D:2 * D + L], erow[:, :], ident[0:L, 0:L]).then_inc(s_wT, 1)
            pe.wait_ge(s_wTc, 3)
            pe.matmul(bank[6][:, 0:L], w1a[:, :], eT[:, :], start=True, stop=True).then_inc(s_pos, 1)
            pe.wait_ge(s_posc, 1)
            pe.sem_inc(s_h, Q)
            with pe.Fori(0, GR) as g:
                pe.wait_ge(s_red, g + 1)
                for s in range(SG):
                    pe.wait_ge(s_oh1, SG * g + s + 1)
                    for t in range(C):
                        last = pe.matmul(bank[4][:, 0:NB], onesb[:, :], oh1[:, s % Q, :, t],
                                         start=(s == 0 and t == 0), stop=(s == SG - 1 and t == C - 1))
                    last.then_inc(s_h, 1)
            pe.wait_ge(s_ls, 1)
            for g in range(GR):
                pe.matmul(bank[5][0:NB + 1, g:g + 1], lstart[0:1, g, :], ones[0:1, 0:1], start=True, stop=True)
                last = pe.matmul(bank[5][0:NB + 1, GR + g:GR + g + 1], dstep[0:1, g, :], ones[0:1, 0:1],
                                 start=True, stop=True)
            last.then_inc(s_lc, 1)
            pe.wait_ge(s_lcc, 1)
            pe.wait_ge(s_tge, 1)
            for n in range(3):
                a, b = n * TW, min(NT, (n + 1) * TW)
                last = pe.matmul(bank[5 + n][0:1, 0:b - a], onesb[0:NB, 0:1], tile_ge[0:NB, a:b], start=True, stop=True)
            last.then_inc(s_tge, 1)
            pe.wait_ge(s_toff, 3)

            def rank_step(n, h):
                pe.wait_ge(s_oh, n + 1)
                pe.wait_ge(s_base, n + 1)
                pe.wait_ge(s_rel, n + 1)
                pe.matmul(octv(h), ones[0:1, 0:P], base[0:1, h, :].unsqueeze(2).broadcast_to([1, NB, C]),
                          start=True, stop=False, skip_group_check=True)
                pe.matmul(octv(h), lower[:, :], oh[:, h, :, :], start=False, stop=False, skip_group_check=True)
                for k in range(1, C):
                    pe.matmul(octv(h)[:, :, k:C], onesb[:, :], oh[:, h, :, 0:C - k], start=False, stop=(k == C - 1),
                              skip_group_check=True)
                for t in range(C):
                    last = pe.matmul(bank[2 + h][:, 0:NB], onesb[:, :], oh[:, h, :, t], start=(t == 0), stop=(t == C - 1))
                last.then_inc(s_rank, 1)

            def permute(n, s):
                r = (s - 2) % Q
                for t in range(C):
                    if t % (C // 2) == 0:
                        pe.wait_ge(s_hp, 2 * n + t // (C // 2) + 1)
                    pe.wait_ge(s_val, C * (n + 2) + t + 2)
                    last = pe.matmul(bank[4][:, 0:2 * LC], at_p[:, r, t, :],
                                     at_c[:, r, t, :, :].rearrange("p w c -> p (w c)"),
                                     start=(s == 2 and t == 0), stop=(s == 1 and t == C - 1),
                                     skip_group_check=True)
                last.then_inc(s_pm, 1)

            pe.wait_ge(s_init, 6)
            pe.matmul(bank[4][:, 0:2 * LC], at_p[:, 2, 0, :], at_c[:, 2, 0, :, :].rearrange("p w c -> p (w c)"),
                      start=True, stop=True)
            pe.sem_inc(s_pm, 2)
            rank_step(0, 0)
            with pe.Fori(0, GR) as g:
                for s in range(SG):
                    n, h = SG * g + s, s % 2
                    rank_step(n + 1, 1 - h)
                    if s == 2:
                        pe.wait_ge(s_gev, g + 1)
                    permute(n, s)
                    if s == 3:
                        pe.wait_ge(s_bg, g + 1)
                        for k in range(NK):
                            last = pe.matmul(bank[7][:, k:k + 1], begun[0:NB + 1, k * P:(k + 1) * P], dsnow[:, :],
                                             start=True, stop=True)
                        last.then_inc(s_dst, 1)
            permute(SG * GR, 0)
            permute(SG * GR + 1, 1)
            pe.wait_ge(s_meta, 32)
            pe.wait_ge(s_rel, 2 + SG * GR)
            for m in range(-(-NT // P)):
                w = min(P, NT - P * m)
                ge(pe, s_mtc, m - 1)
                ge(pe, s_mta, m - 1)
                for q in range(2):
                    last = pe.transpose(bank[2 * q + m % 2][:, 0:w], sorted_rows[0:w, m, :, q], ident[0:w, 0:w])
                last.then_inc(s_mtr, 1)

            def transpose_embeddings(c, h):
                pe.wait_ge(s_ec, c + 1)
                pe.wait_ge(s_ea, c + 1)
                for q in range(2):
                    last = pe.transpose(bank[5 + h][:, q * D:(q + 1) * D], gnr[:, h, q, :], ident[:, :])
                last.then_inc(s_eT, 1)

            def products(layer, c, it, h):
                for u in range(T):
                    j = NT * layer + T * c + u
                    pe.wait_ge(s_g[h * T + u], 16 * ((NST // 2) * layer + it + 1))
                    pe.wait_ge(s_S, j + 1)
                    ge(pe, s_acc, j + 2 - PR)
                    pe.matmul(bank[u % PR][:, 0:BUCKET], msg[:, h * T + u, :], onehot[:, u % SR, :],
                              start=True, stop=True).then_inc(s_mm, 1)

            for layer in range(LAYERS):
                if layer == 1:
                    pe.sem_inc(s_eT, 2)
                for c in range(2):
                    products(layer, c, 0, c)
                    if layer == 1:
                        transpose_embeddings(c, c)
                with pe.Fori(1, LOOP // 2) as i:
                    for h in range(2):
                        products(layer, 2 * i + h, i, h)
                        if layer == 1:
                            transpose_embeddings(2 * i + h, h)
                for c in range(LOOP, NST):
                    products(layer, c, c // 2, c % 2)
                    if layer == 1 and c < NB:
                        transpose_embeddings(c, c % 2)
                pe.wait_ge(s_acc, NT * (layer + 1) + 1)
                if layer == 1:
                    pe.wait_ge(s_ea, NB + 2)
                for g in range(NB):
                    if layer == 0:
                        ge(pe, (s_t1a, s_t1v)[g % 2], g // 2)
                    else:
                        ge(pe, s_g2r, g - 1)
                    for q in range(2):
                        last = pe.transpose(bank[5 + g % 2][:, q * D:(q + 1) * D],
                                            acc[:, (2 * g + q) * D:(2 * g + q + 1) * D], ident[:, :])
                    last.then_inc((s_t1, s_t2)[layer], 1)
            pe.wait_ge(s_g2r, NB)
            for g in range(NB):
                pe.wait_ge(s_gn, g + 1)
                ge(pe, s_gnc, g - 1)
                for q in range(2):
                    last = pe.transpose(bank[5 + g % 2][:, q * D:(q + 1) * D], normed[:, g % NR, q, :], ident[:, :])
                last.then_inc(s_gnT, 1)

            def first_product(bt, k):
                m, w = NG * bt + k, min(LG, L - LG * k)
                pe.wait_ge(s_xc, m + 1)
                ge(pe, s_th, m if bt else m - 1)
                pe.matmul(in_bank(bt, k, 1)[:, 0:w * P], w1b[:, :], xT[:, m % 2, 0:w * P], start=True, stop=True).then_inc(s_z, 1)

            def rows_in(bt, k):
                if bt >= BT:
                    return
                m, w = NG * bt + k, min(LG, L - LG * k)
                pe.wait_ge(s_sq[bt % 2 * NG + k], 16 * (NST + w * (bt // 2 + 1)))
                ge(pe, s_xc, m if bt else m - 1)
                for j in range(w):
                    last = pe.transpose(in_bank(bt, k, 0)[:, j * P:(j + 1) * P], seq[:, bt % 2, LG * k + j, :], ident[:, :])
                last.then_inc(s_x, 1)

            def read_out(bt, k):
                m, w = NG * bt + k, min(LG, L - LG * k)
                pe.wait_ge(s_sg, m + 1)
                ge(pe, s_bm, m - 1)
                for j in range(w):
                    last = pe.matmul(bank[(4, 7)[m % 2]][:, j:j + 1], nh2[:, m % 2, j * P:(j + 1) * P], w2c[:, :],
                                     start=True, stop=True)
                last.then_inc(s_bt, 1)

            def scores(bt, n):
                if bt < 0 or n >= NS:
                    return
                w = 512 if n < NS - 1 else REM
                if n % 2:
                    ge(pe, s_scv, (NS // 2) * bt + n // 2)
                else:
                    ge(pe, s_sca, (-(-NS // 2)) * bt + n // 2)
                pe.matmul(bank[5 + n % 2][:, 0:w], selT[:, :], acc[:, 512 * n:512 * n + w],
                          start=True, stop=True).then_inc(s_sc, 1)

            for k in range(NG):
                rows_in(0, k)
                if k:
                    first_product(0, k - 1)
            first_product(0, NG - 1)
            for w in range(BT + 1):
                if w < BT:
                    pe.wait_ge(s_hs, w + 1)
                    ge(pe, s_bm, NG * w)
                    pe.transpose(bank[4][:, P:2 * P], hrow[:, :], ident[:, :]).then_inc(s_hT, 1)
                    pe.wait_ge(s_hsc, w + 1)
                    pe.matmul(bank[7][:, P:2 * P], g2T[:, :], hsT[:, :], start=True, stop=True).then_inc(s_p2, 1)
                for k in range(NG):
                    if w < BT:
                        m, n = NG * w + k, min(LG, L - LG * k) * P
                        if k == 0 and w == 0:
                            pe.wait_ge(s_th, NG)
                        if k == 1:
                            pe.wait_ge(s_b2, w + 1)
                        if k:
                            read_out(w, k - 1)
                        pe.wait_ge(s_th, m + 1)
                        ge(pe, s_ya, m - 1)
                        pe.matmul(bank[2 + m % 2][:, 0:n], g1T[:, :], nh1[:, k * LG * P:k * LG * P + n],
                                  start=True, stop=True).then_inc(s_y, 1)
                    rows_in(w + 1, k)
                    if w and k == 0:
                        pe.wait_ge(s_sn, 5 * w)
                        pe.transpose(bank[4][:, 2 * P:3 * P], sess[:, 1, :], ident[:, :]).then_inc(s_sT, 1)
                        pe.wait_ge(s_sTc, w)
                        pe.wait_ge(s_gnc, NB)
                    scores(w - 1, 2 * k)
                    if k and w + 1 < BT:
                        first_product(w + 1, k - 1)
                    scores(w - 1, 2 * k + 1)
                if w + 1 < BT:
                    first_product(w + 1, NG - 1)
                if w < BT:
                    read_out(w, NG - 1)


_INS = ["r_items", "r_inputs", "r_alias_inputs", "L0_rec_item_features", "L0_rec_adj_row", "L0_rec_adj_col",
        "L0_rec_adj_val", "L0_rec_emb", "L0_rec_w_1", "L0_rec_w_2", "L0_rec_glu1_w", "L0_rec_glu1_b", "L0_rec_glu2_w"]


def kernel(**inputs):
    import numpy as _np
    import concourse.bacc as _bacc
    from concourse import mybir as _mybir
    from concourse.bass_utils import run_bass_kernel_spmd as _run

    nc = _bacc.Bacc("TRN2", target_bir_lowering=False, num_devices=1)
    arrays, args = {}, []
    for name in _INS:
        a = _np.ascontiguousarray(inputs[name])
        arrays[f"in_{name}"] = a
        args.append(nc.dram_tensor(f"in_{name}", a.shape, _mybir.dt.from_np(a.dtype), kind="ExternalInput").ap())
    shape = (inputs["r_items"].shape[0], inputs["L0_rec_emb"].shape[0])
    args.append(nc.dram_tensor("scores", shape, _mybir.dt.float32, kind="ExternalOutput").ap())
    recommender_program(nc, *args)
    r = _run(nc, [arrays], core_ids=[0])
    return r.results[0]["scores"]
```
